# Optimizing a Trainium2 kernel written in Bass

```python
import numpy as np
import jax
import jax.numpy as jnp

def _softmax(x, axis=-1):
    return jax.nn.softmax(x, axis=axis)

def _gelu(x):
    return jax.nn.gelu(x, approximate=True)

def _silu(x):
    return jax.nn.silu(x)

def _sigmoid(x):
    return jax.nn.sigmoid(x)

def _layernorm(x, axis=-1, eps=1e-05):
    m = jnp.mean(x, axis=axis, keepdims=True)
    v = jnp.var(x, axis=axis, keepdims=True)
    return (x - m) / jnp.sqrt(v + eps)

def _scatter_add(tgt, idx, src, axis=0):
    return tgt.at[idx].add(src)

def _segment_sum(src, seg, n):
    return jax.ops.segment_sum(src, seg, n)
kernel_name = 'mk_prb_d1_jaxref_r4_d96c4e'

def setup_inputs(seed: int=0):
    np.random.seed(seed)
    _w = jnp.asarray

    def _L0_attn_setup():
        import jax, jax.numpy as jnp
        import numpy as np
        D_MODEL = 256
        B, S = (4, 1024)

        def _linear_scan(x_scan, a):

            def combine(l, r):
                al, xl = l
                ar, xr = r
                return (al * ar, ar * xl + xr)
            _, h = jax.lax.associative_scan(combine, (a, x_scan), axis=1)
            return h
        key = jax.random.key(seed)
        ks = jax.random.split(key, 4)
        scale = 1.0 / np.sqrt(D_MODEL)
        return {'x': jax.random.normal(ks[0], (B, S, D_MODEL), dtype=jnp.float32), 'Wg': jax.random.normal(ks[1], (D_MODEL, D_MODEL), dtype=jnp.float32) * scale, 'bg': jnp.zeros((D_MODEL,), dtype=jnp.float32), 'Wv': jax.random.normal(ks[2], (D_MODEL, D_MODEL), dtype=jnp.float32) * scale, 'bv': jnp.zeros((D_MODEL,), dtype=jnp.float32), 'Wd': jax.random.normal(ks[3], (D_MODEL, D_MODEL), dtype=jnp.float32) * scale, 'bd': jnp.ones((D_MODEL,), dtype=jnp.float32)}
    _L0_attn_in = _L0_attn_setup()

    def _L0_ffn_setup():
        import jax, jax.numpy as jnp
        import numpy as np
        B, S, D, E, TOP_K = (2, 256, 256, 8, 2)
        H = 4 * D
        key = jax.random.key(seed)
        ks = jax.random.split(key, 12)
        sc = 0.02
        return {'x': jax.random.normal(ks[0], (B, S, D), jnp.float32), 'Wg': jax.random.normal(ks[1], (E, D), jnp.float32) * sc, 'bg': jnp.zeros((E,), jnp.float32), 'bias': jnp.zeros((E,), jnp.float32), 'W1': jax.random.normal(ks[2], (E, H, D), jnp.float32) * sc, 'b1': jnp.zeros((E, H), jnp.float32), 'W2': jax.random.normal(ks[3], (E, D, H), jnp.float32) * sc, 'b2': jnp.zeros((E, D), jnp.float32), 'Ws1': jax.random.normal(ks[4], (H, D), jnp.float32) * sc, 'bs1': jnp.zeros((H,), jnp.float32), 'Ws2': jax.random.normal(ks[5], (D, H), jnp.float32) * sc, 'bs2': jnp.zeros((D,), jnp.float32)}
    _L0_ffn_in = _L0_ffn_setup()
    _d = {'L0_attn_x': _L0_attn_in['x'], 'L0_attn_Wg': _L0_attn_in['Wg'], 'L0_attn_bg': _L0_attn_in['bg'], 'L0_attn_Wv': _L0_attn_in['Wv'], 'L0_attn_bv': _L0_attn_in['bv'], 'L0_attn_Wd': _L0_attn_in['Wd'], 'L0_attn_bd': _L0_attn_in['bd'], 'L0_ffn_Wg': _L0_ffn_in['Wg'], 'L0_ffn_bg': _L0_ffn_in['bg'], 'L0_ffn_bias': _L0_ffn_in['bias'], 'L0_ffn_W1': _L0_ffn_in['W1'], 'L0_ffn_b1': _L0_ffn_in['b1'], 'L0_ffn_W2': _L0_ffn_in['W2'], 'L0_ffn_b2': _L0_ffn_in['b2'], 'L0_ffn_Ws1': _L0_ffn_in['Ws1'], 'L0_ffn_bs1': _L0_ffn_in['bs1'], 'L0_ffn_Ws2': _L0_ffn_in['Ws2'], 'L0_ffn_bs2': _L0_ffn_in['bs2']}
    _x0 = _d['L0_attn_x']
    _d['L0_attn_x'] = jax.random.normal(jax.random.fold_in(jax.random.key(seed), 1), (8, 512, 256), dtype=_x0.dtype)
    del _x0
    return _d

def reference(L0_attn_x, L0_attn_Wg, L0_attn_bg, L0_attn_Wv, L0_attn_bv, L0_attn_Wd, L0_attn_bd, L0_ffn_Wg, L0_ffn_bg, L0_ffn_bias, L0_ffn_W1, L0_ffn_b1, L0_ffn_W2, L0_ffn_b2, L0_ffn_Ws1, L0_ffn_bs1, L0_ffn_Ws2, L0_ffn_bs2):

    def _L0_attn_ref(x, Wg, bg, Wv, bv, Wd, bd):
        import jax, jax.numpy as jnp
        import numpy as np
        D_MODEL = 256
        B, S = (4, 1024)

        def _linear_scan(x_scan, a):

            def combine(l, r):
                al, xl = l
                ar, xr = r
                return (al * ar, ar * xl + xr)
            _, h = jax.lax.associative_scan(combine, (a, x_scan), axis=1)
            return h
        g = jnp.einsum('bsd,de->bse', x, Wg) + bg
        v = jnp.einsum('bsd,de->bse', x, Wv) + bv
        d = jnp.einsum('bsd,de->bse', x, Wd) + bd
        x_scan = jax.nn.sigmoid(g) * jnp.tanh(v)
        a = 0.001 + 0.998 * jax.nn.sigmoid(d)
        return _linear_scan(x_scan, a)

    def _L0_ffn_ref(x, Wg, bg, bias, W1, b1, W2, b2, Ws1, bs1, Ws2, bs2):
        import jax, jax.numpy as jnp
        import numpy as np
        B, S, D, E, TOP_K = (2, 256, 256, 8, 2)
        H = 4 * D
        b, s, d = x.shape
        xf = x.reshape(-1, d)
        T = xf.shape[0]
        scores = jax.nn.sigmoid(xf @ Wg.T + bg + bias)
        top_scores, top_idx = jax.lax.top_k(scores, TOP_K)
        weights = jnp.zeros((T, E), scores.dtype)
        weights = weights.at[jnp.arange(T)[:, None], top_idx].add(top_scores)
        h = jax.nn.gelu(jnp.einsum('td,ehd->teh', xf, W1) + b1, approximate=False)
        eo = jnp.einsum('teh,edh->ted', h, W2) + b2
        combined = jnp.einsum('ted,te->td', eo, weights)
        shared = jax.nn.gelu(xf @ Ws1.T + bs1, approximate=False) @ Ws2.T + bs2
        return (shared + combined).reshape(b, s, d)
    x = L0_attn_x
    xn = _layernorm(x, axis=-1)
    x = x + _L0_attn_ref(xn, L0_attn_Wg, L0_attn_bg, L0_attn_Wv, L0_attn_bv, L0_attn_Wd, L0_attn_bd) + _L0_ffn_ref(xn, L0_ffn_Wg, L0_ffn_bg, L0_ffn_bias, L0_ffn_W1, L0_ffn_b1, L0_ffn_W2, L0_ffn_b2, L0_ffn_Ws1, L0_ffn_bs1, L0_ffn_Ws2, L0_ffn_bs2)
    return x

_drawn_inputs = setup_inputs


def setup_inputs(seed=0):
    import zlib

    import numpy as np

    out = dict(_drawn_inputs(seed))
    spreads = {'L0_attn_bg': (0.0, 0.471),
     'L0_attn_bv': (0.0, 0.1),
     'L0_attn_bd': (1.0, 0.2),
     'L0_ffn_bg': (0.0, 0.1),
     'L0_ffn_bias': (0.0, 0.1),
     'L0_ffn_b1': (0.0, 0.31),
     'L0_ffn_b2': (0.0, 0.1),
     'L0_ffn_bs1': (0.0, 0.268),
     'L0_ffn_bs2': (0.0, 0.1)}
    factors = {}
    for name, (base, spread) in spreads.items():
        noise = np.random.default_rng([zlib.crc32(name.encode()), seed]).standard_normal(out[name].shape)
        drawn = base * np.exp(spread * noise) if base else spread * noise
        out[name] = jnp.asarray(drawn.astype(out[name].dtype))
    for name, factor in factors.items():
        out[name] = (out[name] * factor).astype(out[name].dtype)
    return out
```

```python
from contextlib import ExitStack, contextmanager

import concourse.bass as bass
from concourse import mybir

F32, F16, I32, U32 = mybir.dt.float32, mybir.dt.float16, mybir.dt.int32, mybir.dt.uint32
ALU, ACT, AX = mybir.AluOpType, mybir.ActivationFunctionType, mybir.AxisListType
RMAX, RADD = bass.bass_isa.ReduceOp.max, bass.bass_isa.ReduceOp.add

P = 128
SEQS, SEQ, D, H, E = 8, 512, 256, 1024, 8
TOKENS = SEQS * SEQ
TILES = TOKENS // P
TPB = SEQ // P
KD, KH = D // P, H // P
ROWS = 256
ROUTED = 2 * TOKENS // ROWS + E - 1
LEAD = 8
SHARED = TOKENS // ROWS
TRAIL = SHARED - LEAD
SLOTS = LEAD + ROUTED + TRAIL
NW = E + 1
WSET = 4 * KD * H
HALF = KD * H
GATES = 3 * D
GCOL = GATES + E
QR = ROUTED * 2
QALL = SLOTS * 2
XSCALE = 256.0
TOP = 2.0 ** 14
EXPONENT = 0x7F800000
EPS = 1e-5
RING = 4
AHEAD = 2
PAR = 12


class Tally:

    def __init__(self, eng, sem):
        self.eng, self.sem, self.base, self.k = eng, sem, 0, 0

    def mark(self, ins):
        ins.then_inc(self.sem, 1)
        self.k += 1

    def settle(self):
        self.eng.wait_ge(self.sem, self.base + self.k)

    @contextmanager
    def loop(self, trips, per):
        start = self.k
        assert not self.base
        with self.eng.Fori(0, trips) as i:
            self.base, self.k = i * per + start, 0
            yield i
            assert self.k == per, self.k
        self.base, self.k = 0, start + trips * per


def layer(nc, x, w1, w2, gates, b1, b2, gbias, sbias, out):
    ctx = ExitStack()
    with ctx:
        def sb(name, shape, dt):
            return ctx.enter_context(nc.sbuf_tensor(name, shape, dt))

        def sem(name):
            return ctx.enter_context(nc.semaphore(name))

        xhl_dram = nc.dram_tensor("xhl_rows", (TOKENS, 2 * D), F16, kind="Internal").ap()
        r_dram = nc.dram_tensor("r_rows", (TOKENS, D), F32, kind="Internal").ap()
        y_dram = nc.dram_tensor("y_rows", (ROUTED * ROWS, D), F32, kind="Internal").ap()
        ys_dram = nc.dram_tensor("shared_rows", (TOKENS, D), F32, kind="Internal").ap()
        list_dram = nc.dram_tensor("row_tokens", (P * QR, 1), U32, kind="Internal").ap()

        W = sb("W", [P, NW * WSET], F16)
        PT = sb("PT", [P, NW, PAR + D], F32)
        par = [sb(f"par{i}", [P, PAR + D], F32) for i in range(2)]
        stage = [sb(f"stage{i}", [P, HALF], F32) for i in range(2)]
        xg = [sb(f"xg{i}", [P, 2, 2 * D], F16) for i in range(2)]
        xgT = [sb(f"xgT{i}", [P, 4, ROWS], F16) for i in range(2)]
        arena = sb("arena", [P, 6144], F32)
        small = sb("small", [P, 256], F32)
        starts_i = sb("starts_i", [P, ROUTED], I32)[:, :]
        ident = sb("ident", [P, P], F16)
        identf = sb("identf", [P, P], F32)
        before = sb("before", [P, P], F16)
        ones = sb("ones", [P, P], F16)
        idx = sb("idx", [P, QALL], U32)
        idx_now = [sb(f"idx_now{i}", [P, 2], U32) for i in range(2)]
        slot_set = sb("slot_set", [P, SLOTS], I32)
        token = sb("token", [P, TILES], U32)
        top_w = sb("top_w", [P, 2, TILES], F32)
        y_row = sb("y_row", [P, 2, TILES], U32)
        l_row = sb("l_row", [P, 2, TILES], U32)
        sidx = [sb(f"sidx{i}", [P, 4], U32) for i in range(2)]

        xt = [arena[:, i * 1024:(i + 1) * 1024] for i in range(2)]
        xs = arena[:, 2048:3072]
        sg = [arena[:, 3072 + i * 512:3584 + i * 512] for i in range(2)]
        tv = [arena[:, 4096 + i * 512:4608 + i * 512] for i in range(2)]
        dec = [arena[:, 5120 + i * 512:5632 + i * 512] for i in range(2)]
        last = (NW - 1) * WSET
        gw = W[:, last:last + 2 * KD * GCOL].rearrange("p (s c n) -> p s c n", s=2, c=KD)
        gw_flat = W[:, last:last + 2 * KD * GCOL].rearrange("p (s n) -> p s n", s=2)
        at = last + 2 * KD * GCOL
        xTA = W[:, at:at + 4 * SEQ].rearrange("p (q n) -> p q n", q=4)
        xhl = W[:, at + 4 * SEQ:at + 8 * SEQ].rearrange("p (t n) -> p t n", t=TPB)
        h32 = [arena[:, i * ROWS:(i + 1) * ROWS] for i in range(RING)]
        hhl = [arena[:, 1024 + i * ROWS:1024 + (i + 1) * ROWS].bitcast(F16).rearrange(
            "p (s n) -> p s n", s=2) for i in range(RING)]
        y_sb = [arena[:, 2048 + i * 512:2560 + i * 512] for i in range(2)]
        yg = [stage[i][:, 0:1024].rearrange("p (t k n) -> p t k n", t=2, k=2) for i in range(2)]
        racc = [stage[i][:, 1024:1536] for i in range(2)]
        ysh = [stage[i][:, 1536:2048] for i in range(2)]

        def table(i):
            return arena[:, 256 * i:256 * (i + 1)].rearrange("p (t e) -> p t e", e=E)

        logit, score = arena[:, 0:256], arena[:, 256:512]
        S, eq, key, oh1, oh2, S2, cum, rank, pos, tmp, desc = (table(i) for i in range(1, 12))
        mask = arena[:, 3072:3200].bitcast(F16)
        row1 = arena[:, 3200:3232]
        best = arena[:, 3264:3296]
        row_i = arena[:, 3328:3360].bitcast(I32)
        row_lo = arena[:, 3392:3424].bitcast(I32)
        row_hi = arena[:, 3456:3488].bitcast(I32)
        starts = arena[:, 3520:3520 + ROUTED]
        cmp_ = arena[:, 3584:3584 + ROUTED * E].rearrange("p (i e) -> p i e", e=E)
        sets = arena[:, 3904:3904 + ROUTED]
        one = arena[:, 3968:4000]

        stats = small[:, 0:24].rearrange("p (t n) -> p t n", t=TPB)
        mv = small[:, 24:32].rearrange("p (t n) -> p t n", t=TPB)
        ve, rs, neghalf, half = small[:, 32:36], small[:, 36:40], small[:, 40:44], small[:, 44:46]
        ssq, ssum, norm = small[:, 46:48], small[:, 48:50], small[:, 50:53]
        pw, ip, scl, inv = small[:, 56:59], small[:, 60:63], small[:, 64:67], small[:, 68:71]
        a_gate = small[:, 72:73]
        b1max = small[:, 80:89]
        b1red = small[:, 90:99]
        gb = small[:, 100:108]
        gb2 = small[:, 108:116]
        sbt = small[:, 116:122]
        count = small[:, 124:132]
        count_i = small[:, 132:140].bitcast(I32)
        pad_i = small[:, 140:148].bitcast(I32)
        pad = small[:, 148:156]
        pad_end = small[:, 156:164]
        base = small[:, 164:172]
        scratch, scratch_p = small[:, 172:173], small[:, 174:176]

        bank = [ctx.enter_context(nc.psum_tensor(f"bank{i}", [P, 512], F32)) for i in range(8)]
        ps_xT = [bank[i][:, :].bitcast(F16) for i in (0, 1)]
        ps_g = [bank[2], bank[3], bank[4]]
        ps_r = [bank[5], bank[6]]
        ps_log = bank[7]
        ps_h = [bank[i] for i in range(4)]
        ps_y = [bank[4], bank[5]]
        ps_s = bank[6][:, :].bitcast(F16).rearrange("p (q n) -> p q n", q=4)

        x_in = [sem(f"x_in{i}") for i in range(2)]
        w_in = [sem(f"w_in{i}") for i in range(2)]
        tab_in = sem("tab_in")
        const_ok = sem("const_ok")
        stage_used = [sem(f"stage_used{i}") for i in range(2)]
        ssq_ok = sem("ssq_ok")
        norm_ok = sem("norm_ok")
        scale_ok = sem("scale_ok")
        whi_ok = sem("whi_ok")
        var_ok = sem("var_ok")
        rs_ok = sem("rs_ok")
        xs_ok = sem("xs_ok")
        xhi_ok = sem("xhi_ok")
        xhl_ok = sem("xhl_ok")
        xhl_out = sem("xhl_out")
        xT_ps = sem("xT_ps")
        xT_ok = sem("xT_ok")
        logit_ok = sem("logit_ok")
        proj_ps = sem("proj_ps")
        proj_act = sem("proj_act")
        scan_ok = sem("scan_ok")
        scanT_ps = sem("scanT_ps")
        r_ok = sem("r_ok")
        r_out = [sem(f"r_out{i}") for i in range(2)]
        dve_own = sem("dve_own")
        pool_own = sem("pool_own")
        lg_ok = sem("lg_ok")
        sig_ok = sem("sig_ok")
        mask_ok = sem("mask_ok")
        rank_ps = sem("rank_ps")
        route_ok = sem("route_ok")
        zero_out = sem("zero_out")
        list_out = [sem(f"list_out{i}") for i in range(2)]
        list_in = sem("list_in")
        rows_in = [sem(f"rows_in{i}") for i in range(2)]
        rowsT_ps = sem("rowsT_ps")
        rowsT_ok = sem("rowsT_ok")
        par_ok = sem("par_ok")
        h_ps = sem("h_ps")
        gelu_ok = sem("gelu_ok")
        hhl_ok = sem("hhl_ok")
        y_ps = sem("y_ps")
        y_ok = sem("y_ok")
        y_out = [sem(f"y_out{i}") for i in range(2)]
        fin_in = [sem(f"fin_in{i}") for i in range(2)]
        fin_ok = sem("fin_ok")
        o_out = [sem(f"o_out{i}") for i in range(2)]

        block = ctx.enter_context(nc.Block())

        x_v = x.rearrange("(b t p) d -> b p t d", t=TPB, p=P)
        xhl_v = xhl_dram.rearrange("(b t p) d -> b p t d", t=TPB, p=P)
        r_v = r_dram.rearrange("(b t p) d -> b p t d", t=TPB, p=P)
        w1_v = w1.rearrange("e (c p) h -> e p c h", p=P)
        w2_v = w2.rearrange("e (j p) d -> e p j d", p=P)
        y_v = y_dram.rearrange("(s t p) d -> s p t d", t=2, p=P)
        ys_v = ys_dram.rearrange("(s t p) d -> s p t d", t=2, p=P)
        rf_v = r_dram.rearrange("(s t p) d -> s p t d", t=2, p=P)
        out_v = out.rearrange("(s t p) d -> s p t d", t=2, p=P)

        def chunks(ap, n):
            return ap.rearrange("p (t n) -> p t n", t=n)

        def at1(v, n):
            return v[bass.ds(n, 1)].rearrange("a p t d -> (a p) t d")

        @block.sync
        def _(sp):
            def load_x(b, u):
                sp.dma_start(chunks(xt[u], TPB), at1(x_v, b)).then_inc(x_in[u], 16)

            def load_w(layer_, n):
                sp.dma_start(chunks(stage[layer_][:, :], (KD, KH)[layer_]),
                             at1((w1_v, w2_v)[layer_], n)).then_inc(w_in[layer_], 16)

            load_x(0, 0)
            sp.dma_start(chunks(stage[0][:, 0:KD * GCOL], KD),
                         gates.rearrange("(c p) n -> p c n", p=P)).then_inc(w_in[0], 16)
            load_w(1, 0)
            load_x(1, 1)
            sp.dma_start(PT[:, :, 4:PAR], b1).then_inc(tab_in, 16)
            sp.dma_start(PT[:, :, PAR:PAR + D], b2.partition_broadcast(P)).then_inc(tab_in, 16)
            sp.dma_start(gb, gbias[0].partition_broadcast(P)).then_inc(tab_in, 16)
            sp.dma_start(gb2, gbias[1].partition_broadcast(P)).then_inc(tab_in, 16)
            sp.dma_start(sbt, sbias).then_inc(tab_in, 16)
            sp.wait_ge(stage_used[0], 1)
            load_w(0, 0)

            def batch(b, u, more):
                sp.wait_ge(xhl_ok, b + 1)
                sp.dma_start(at1(xhl_v, b), xhl).then_inc(xhl_out, 16)
                for l in range(2):
                    sp.wait_ge(stage_used[l], b + 2 - l)
                    load_w(l, b + 1)
                sp.wait_ge(r_ok, b + 2)
                sp.dma_start(at1(r_v, b), chunks(xt[u], TPB)).then_inc(r_out[u], 16)
                if more:
                    sp.wait_ge(r_out[u], (b - u) * 8 + 16)
                    load_x(b + 2, u)

            for b in range(SEQS):
                batch(b, b % 2, b + 2 < SEQS)

            def store_y(n, u, to, row):
                sp.wait_ge(y_ok, n + 3)
                sp.dma_start(at1(to, row), chunks(y_sb[u], 2)).then_inc(y_out[u], 16)

            with sp.Fori(0, LEAD // 2) as it:
                for u in range(2):
                    store_y(it * 2 + u, u, ys_v, it * 2 + u)
            with sp.Fori(0, ROUTED // 2) as it:
                for u in range(2):
                    store_y(it * 2 + LEAD + u, u, y_v, it * 2 + u)
            store_y(LEAD + ROUTED - 1, 0, y_v, ROUTED - 1)

            def store_out(m, u):
                sp.wait_ge(fin_ok, m + 1)
                sp.dma_start(at1(out_v, m), chunks(racc[u], 2)).then_inc(o_out[u], 16)

            for w in range(2):
                store_out(w, w)
            with sp.Fori(0, TRAIL // 2 - 1) as it:
                for v in range(2):
                    store_y(it * 2 + LEAD + ROUTED + v, 1 - v, ys_v, it * 2 + LEAD + v)
                    for w in range(2):
                        store_out((it * 2 + v) * 2 + 2 + w, w)
            for v in range(2):
                store_y(SLOTS - 2 + v, 1 - v, ys_v, SHARED - 2 + v)
            for w in range(2):
                store_out(SHARED - 2 + w, w)
            for u in range(2):
                sp.wait_ge(o_out[u], 16 * SHARED // 2)
                sp.wait_ge(y_out[u], 16 * ((SLOTS + 1 - u) // 2))

        @block.gpsimd
        def _(pool):
            own = Tally(pool, pool_own)

            def made(ins):
                own.mark(ins)

            def hold():
                pool.tensor_tensor(out=scratch_p, in0=half, in1=half, op=ALU.mult)

            made(pool.memset(ident[:, :], 0.0))
            made(pool.memset(identf[:, :], 0.0))
            made(pool.memset(before[:, :], 0.0))
            pool.memset(ones[:, :], 1.0).then_inc(const_ok, 1)
            made(pool.memset(neghalf, -0.5))
            made(pool.memset(half, 0.5))
            own.settle()
            for m in (ident, identf):
                pool.affine_select(out=m[:, :], in_=m[:, :], compare_op=ALU.not_equal, fill=1.0, base=0,
                                   pattern=[[-1, P]], channel_multiplier=1).then_inc(const_ok, 1)
            pool.affine_select(out=before[:, :], in_=before[:, :], compare_op=ALU.is_ge, fill=1.0, base=0,
                               pattern=[[-1, P]], channel_multiplier=1).then_inc(const_ok, 1)
            made(pool.iota(token[:, :], pattern=[[P, TILES]], base=0, channel_multiplier=1))
            made(pool.iota(starts_i, pattern=[[ROWS, ROUTED]], base=0, channel_multiplier=0))
            made(pool.iota(idx[:, 0:2 * LEAD], pattern=[[P, 2 * LEAD]], base=0, channel_multiplier=1))
            made(pool.iota(idx[:, 2 * (LEAD + ROUTED):QALL], pattern=[[P, 2 * TRAIL]], base=LEAD * ROWS,
                           channel_multiplier=1))
            made(pool.memset(idx[:, 2 * LEAD:2 * (LEAD + ROUTED)], 0))
            own.settle()
            pool.dma_start(list_dram.rearrange("(p q) a -> p (q a)", p=P),
                           idx[:, 2 * LEAD:2 * (LEAD + ROUTED)]).then_inc(zero_out, 16)
            pool.wait_ge(tab_in, 80)
            pool.wait_ge(scale_ok, 1)
            made(pool.partition_all_reduce(b1red, b1max, P, RMAX))
            own.settle()

            def norms(n):
                pool.wait_ge(ssq_ok, n + 1)
                hold()
                made(pool.partition_all_reduce(ssum, ssq, P, RADD))
                own.settle()
                pool.tensor_tensor(out=norm[:, 0:2], in0=ssum, in1=half, op=ALU.pow).then_inc(norm_ok, 1)

            def rstd(b):
                pool.wait_ge(var_ok, b + 1)
                pool.tensor_tensor(out=rs, in0=ve, in1=neghalf, op=ALU.pow).then_inc(rs_ok, 1)

            rstd(0)
            norms(0)
            with own.loop(SEQS - 1, 1) as b:
                norms(b + 1)
                rstd(b + 1)
            norms(SEQS)
            norms(SEQS + 1)

            def gather_rows(n, u, wait=True):
                if wait:
                    pool.wait_ge(rowsT_ps, n - 1)
                made(pool.tensor_copy(idx_now[u][:, :], idx[:, bass.ds(n * 2, 2)]))
                own.settle()
                hold()
                for t in range(2):
                    pool.indirect_dma_start(
                        xg[u][:, t, :], None, xhl_dram,
                        bass.IndirectOffsetOnAxis(ap=idx_now[u][:, t:t + 1], axis=0)).then_inc(rows_in[u], 16)

            pool.wait_ge(xhl_out, 16 * SEQS)
            pool.wait_ge(zero_out, 16)
            gather_rows(0, 0, wait=False)
            gather_rows(1, 1, wait=False)
            pool.wait_ge(route_ok, 1)

            def scatter(m, u):
                made(pool.tensor_copy(sidx[u][:, 0:2], l_row[:, 0, bass.ds(m * 2, 2)]))
                made(pool.tensor_copy(sidx[u][:, 2:4], l_row[:, 1, bass.ds(m * 2, 2)]))
                made(pool.tensor_copy(tok_now[u], token[:, bass.ds(m * 2, 2)]))
                own.settle()
                hold()
                for k in range(2):
                    for t in range(2):
                        pool.indirect_dma_start(
                            list_dram, bass.IndirectOffsetOnAxis(ap=sidx[u][:, 2 * k + t:2 * k + t + 1], axis=0),
                            tok_now[u][:, t:t + 1], None).then_inc(list_out[u], 16)

            tok_now = [small[:, 200 + 2 * u:202 + 2 * u].bitcast(U32) for u in range(2)]
            scatter(0, 0)
            scatter(1, 1)
            assert TILES // 4 == LEAD
            with own.loop(LEAD // 2 - 1, 2 * 1 + 4 * 3) as it:
                for u in range(2):
                    gather_rows(it * 2 + 2 + u, u)
                    for v in range(2):
                        pool.wait_ge(list_out[v], (it * 2 + u + 1) * 64)
                        scatter((it * 2 + u) * 2 + 2 + v, v)
            for u in range(1):
                for v in range(2):
                    pool.wait_ge(list_out[v], (LEAD - 2 + u + 1) * 64)
                    scatter((LEAD - 2 + u) * 2 + 2 + v, v)
            for v in range(2):
                pool.wait_ge(list_out[v], 64 * LEAD)
            pool.dma_start(idx[:, 2 * LEAD:2 * (LEAD + ROUTED)],
                           list_dram.rearrange("(p q) a -> p (q a)", p=P)).then_inc(list_in, 16)
            pool.wait_ge(list_in, 16)
            sent = SLOTS - TRAIL + 3
            with own.loop((sent - LEAD) // 2, 2) as it:
                for u in range(2):
                    gather_rows(it * 2 + LEAD + u, u)

            def fetch(m, u):
                made(pool.tensor_copy(sidx[u][:, 0:2], y_row[:, 0, bass.ds(m * 2, 2)]))
                made(pool.tensor_copy(sidx[u][:, 2:4], y_row[:, 1, bass.ds(m * 2, 2)]))
                own.settle()
                hold()
                for t in range(2):
                    for k in range(2):
                        pool.indirect_dma_start(
                            yg[u][:, t, k, :], None, y_dram,
                            bass.IndirectOffsetOnAxis(ap=sidx[u][:, 2 * k + t:2 * k + t + 1], axis=0)
                        ).then_inc(fin_in[u], 16)
                pool.dma_start(chunks(racc[u], 2), at1(rf_v, m)).then_inc(fin_in[u], 16)

            def fetch_shared(m, u):
                pool.dma_start(chunks(ysh[u], 2), at1(ys_v, m)).then_inc(fin_in[u], 16)

            pool.wait_ge(y_out[0], 16 * 24)
            pool.wait_ge(y_out[1], 16 * 23)
            for u in range(2):
                pool.wait_ge(r_out[u], 16 * SEQS // 2)
            for m in range(2):
                fetch(m, m)
                fetch_shared(m, m)
            for i in range(TRAIL - 1):
                if sent + i < SLOTS:
                    gather_rows(sent + i, (sent + i) % 2)
                for u in range(2):
                    m = 2 * i + 2 + u
                    pool.wait_ge(o_out[u], 16 * (m // 2))
                    fetch(m, u)
                    n = m if m < LEAD else m + ROUTED
                    pool.wait_ge(y_out[n % 2], 16 * (n // 2 + 1))
                    fetch_shared(m, u)

        @block.scalar
        def _(act):
            def squares(n):
                if n is None:
                    act.wait_ge(w_in[0], 16)
                    nc.scalar.activation(gw_flat[:, 0, :], stage[0][:, 0:KD * GCOL], ACT.Square,
                                         accum_out=ssq[:, 0:1])
                    nc.scalar.activation(ssq[:, 1:2], stage[0][:, 0:1], ACT.Square).then_inc(ssq_ok, 1)
                    return
                for l in range(2):
                    act.wait_ge(w_in[l], (n + 2 - l) * 16)
                    act.wait_ge(norm_ok, n + 1)
                    o = n * WSET + l * 2 * HALF
                    ins = nc.scalar.activation(W[:, bass.ds(o, HALF)], stage[l][:, :], ACT.Square,
                                               accum_out=ssq[:, l:l + 1])
                ins.then_inc(ssq_ok, 1)

            def high_parts(n):
                act.wait_ge(scale_ok, n + 3)
                for l in range(2):
                    o = n * WSET + l * 2 * HALF
                    nc.scalar.activation(W[:, bass.ds(o, HALF)], stage[l][:, :], ACT.Copy,
                                         scale=scl[:, l:l + 1]).then_inc(whi_ok, 1)

            def x_high(b):
                act.wait_ge(xs_ok, b + 1)
                nc.scalar.activation(xhl[:, :, 0:D], chunks(xs, TPB), ACT.Copy).then_inc(xhi_ok, 1)

            def x_T(b):
                act.wait_ge(xT_ps, b + 1)
                for i in range(2):
                    ins = nc.scalar.activation(xTA[:, 2 * i:2 * i + 2, :], chunks(ps_xT[i], 2), ACT.Copy)
                ins.then_inc(xT_ok, 1)

            def projections(b):
                for ch in range(KD):
                    act.wait_ge(scan_ok, b * 2 + ch + 1)
                    act.wait_ge(scanT_ps, b * 2 + ch + 1)
                    for g, (dst, f) in enumerate(((sg, ACT.Sigmoid), (tv, ACT.Tanh), (dec, ACT.Sigmoid))):
                        act.wait_ge(proj_ps, b * 6 + 3 * ch + g + 1)
                        nc.scalar.activation(dst[ch], ps_g[g][:, :], f, bias=sbt[:, 2 * g + ch:2 * g + ch + 1],
                                             scale=a_gate).then_inc(proj_act, 1)

            act.nop().then_inc(proj_act, 3)
            act.nop().then_inc(gelu_ok, RING)
            squares(None)
            act.wait_ge(scale_ok, 2)
            nc.scalar.activation(gw_flat[:, 0, :], stage[0][:, 0:KD * GCOL], ACT.Copy,
                                 scale=scl[:, 0:1]).then_inc(whi_ok, 1)
            x_high(0)
            x_T(0)
            squares(0)
            with act.Fori(0, SEQS - 1) as b:
                high_parts(b)
                act.wait_ge(xhl_out, (b + 1) * 16)
                x_high(b + 1)
                projections(b)
                x_T(b + 1)
                squares(b + 1)
            high_parts(SEQS - 1)
            projections(SEQS - 1)
            act.wait_ge(xhl_out, 16 * SEQS)
            act.wait_ge(proj_ps, 6 * SEQS)
            squares(SEQS)
            act.wait_ge(lg_ok, 1)
            nc.scalar.activation(score, logit, ACT.Sigmoid).then_inc(sig_ok, 1)
            high_parts(SEQS)

            def gelus(n, u):
                act.wait_ge(par_ok, n + 1)
                for j in range(KH):
                    act.wait_ge(h_ps, n * KH + j + 1)
                    act.wait_ge(hhl_ok, n * KH + j + 1)
                    nc.scalar.activation(h32[j % RING], ps_h[j % RING][:, 0:ROWS], ACT.Gelu,
                                         bias=par[u][:, 4 + j:5 + j], scale=par[u][:, 0:1]).then_inc(gelu_ok, 1)

            with act.Fori(0, SLOTS // 2) as it:
                for u in range(2):
                    gelus(it * 2 + u, u)
            gelus(SLOTS - 1, 0)

        @block.vector
        def _(dve):
            own = Tally(dve, dve_own)
            V = nc.vector

            def seq(ins):
                own.mark(ins)
                own.settle()

            dve.wait_ge(tab_in, 80)
            V.tensor_reduce(b1max, PT[:, :, 4:PAR], AX.X, ALU.max, apply_absolute_value=True).then_inc(scale_ok, 1)
            own.mark(V.memset(PT[:, :, 3:4], 0.0))
            seq(V.tensor_tensor(gb, gb, gb2, ALU.add))
            V.engine_nop().then_inc(scan_ok, 2)
            V.engine_nop().then_inc(r_ok, 1)

            def scales(n):
                dve.wait_ge(norm_ok, 1 if n is None else n + 2)
                seq(V.tensor_scalar(norm[:, 2:3], norm[:, 0:1], 16.0,
                                    b1red[:, 0:1] if n is None else b1red[:, bass.ds(n, 1)], ALU.mult, ALU.add))
                seq(V.tensor_scalar(pw, norm, 1e-12, None, ALU.max))
                seq(V.tensor_scalar(pw.bitcast(I32), pw.bitcast(I32), EXPONENT, None, ALU.bitwise_and))
                seq(V.reciprocal(ip, pw))
                seq(V.tensor_scalar(inv, pw, 1.0 / TOP, None, ALU.mult))
                own.mark(V.tensor_scalar(scl, ip, TOP, None, ALU.mult))
                if n is None:
                    V.tensor_scalar(a_gate, inv[:, 0:1], 1.0 / XSCALE, None, ALU.mult).then_inc(scale_ok, 1)
                    return
                own.settle()
                own.mark(V.tensor_scalar(PT[:, bass.ds(n, 1), 0:1].squeeze(1), inv[:, 0:1], 1.0 / XSCALE, None,
                                         ALU.mult))
                own.mark(V.tensor_copy(PT[:, bass.ds(n, 1), 1:2].squeeze(1), scl[:, 2:3]))
                V.tensor_tensor(PT[:, bass.ds(n, 1), 2:3].squeeze(1), inv[:, 1:2], inv[:, 2:3],
                                ALU.mult).then_inc(scale_ok, 1)

            def low_part(n, l):
                o = n * WSET + l * 2 * HALF
                dve.wait_ge(whi_ok, n * 2 + 2 + l)
                V.scalar_tensor_tensor(out=W[:, bass.ds(o + HALF, HALF)], in0=stage[l][:, :], scalar=scl[:, l:l + 1],
                                       in1=W[:, bass.ds(o, HALF)], op0=ALU.mult,
                                       op1=ALU.subtract).then_inc(stage_used[l], 1)

            def variances(b, u):
                dve.wait_ge(x_in[u], (b - u) * 8 + 16)
                for t in range(TPB):
                    own.mark(V.bn_stats(stats[:, t, :], xt[u][:, t * D:(t + 1) * D]))
                own.settle()
                V.memset(scratch, 0.0)
                for t in range(TPB):
                    own.mark(V.bn_aggr(mv[:, t, :], stats[:, t, :]))
                own.settle()
                V.tensor_scalar(ve.unsqueeze(2), mv[:, :, 1:2], EPS, XSCALE ** -2, ALU.add,
                                ALU.mult).then_inc(var_ok, 1)

            def normed(b, u):
                dve.wait_ge(rs_ok, b + 1)
                for t in range(TPB):
                    ins = V.tensor_scalar(xs[:, t * D:(t + 1) * D], xt[u][:, t * D:(t + 1) * D], mv[:, t, 0:1],
                                          rs[:, t:t + 1], ALU.subtract, ALU.mult)
                ins.then_inc(xs_ok, 1)

            def x_low(b):
                dve.wait_ge(xhi_ok, b + 1)
                V.tensor_tensor(xhl[:, :, D:2 * D], chunks(xs, TPB), xhl[:, :, 0:D],
                                ALU.subtract).then_inc(xhl_ok, 1)

            def scans(b):
                for ch in range(KD):
                    dve.wait_ge(proj_act, b * 6 + 3 * ch + 3 + 3)
                    own.mark(V.tensor_tensor(sg[ch], sg[ch], tv[ch], ALU.mult))
                    own.mark(V.tensor_scalar(dec[ch], dec[ch], 0.998, 0.001, ALU.mult, ALU.add))
                    own.settle()
                    V.tensor_tensor_scan(tv[ch], dec[ch], sg[ch], 0.0, ALU.mult, ALU.add).then_inc(scan_ok, 1)

            def residual(b, u):
                dve.wait_ge(scanT_ps, b * 2 + 2 + 2)
                for i in range(2):
                    half_ = xt[u][:, i * 512:(i + 1) * 512]
                    ins = V.tensor_tensor(half_, half_, ps_r[i][:, :], ALU.add)
                ins.then_inc(r_ok, 1)

            def batch(b, u, more):
                scales(b)
                if more:
                    variances(b + 1, 1 - u)
                low_part(b, 0)
                if more:
                    normed(b + 1, 1 - u)
                low_part(b, 1)
                if more:
                    x_low(b + 1)
                scans(b)
                residual(b, u)

            variances(0, 0)
            normed(0, 0)
            scales(None)
            dve.wait_ge(whi_ok, 1)
            V.scalar_tensor_tensor(out=gw_flat[:, 1, :], in0=stage[0][:, 0:KD * GCOL], scalar=scl[:, 0:1],
                                   in1=gw_flat[:, 0, :], op0=ALU.mult, op1=ALU.subtract).then_inc(stage_used[0], 1)
            x_low(0)
            with own.loop(SEQS // 2 - 1, 2 * (8 + 8 + 4)) as it:
                for u in range(2):
                    batch(it * 2 + u, u, True)
            batch(SEQS - 2, 0, True)
            batch(SEQS - 1, 1, False)

            dve.wait_ge(logit_ok, SEQS)
            dve.wait_ge(r_out[0], 16 * SEQS // 2)
            dve.wait_ge(r_out[1], 16 * SEQS // 2)
            V.scalar_tensor_tensor(out=logit.rearrange("p (t e) -> p t e", e=E),
                                   in0=ps_log[:, 0:256].rearrange("p (t e) -> p t e", e=E), scalar=a_gate,
                                   in1=gb.unsqueeze(1).to_broadcast([P, TILES, E]), op0=ALU.mult,
                                   op1=ALU.add).then_inc(lg_ok, 1)
            for e in range(E):
                own.mark(V.memset(desc[:, :, e], float(E - e)))
            own.mark(V.memset(one, 1.0))
            own.mark(V.tensor_copy(starts, starts_i))
            own.mark(V.memset(slot_set[:, :], 0))
            scales(SEQS)
            low_part(SEQS, 0)
            low_part(SEQS, 1)
            dve.wait_ge(sig_ok, 1)

            def wide(v):
                return v.unsqueeze(2).to_broadcast([P, TILES, E])

            for k, (src, oh) in enumerate(((S, oh1), (S2, oh2))):
                seq(V.tensor_reduce(top_w[:, k, :], src, AX.X, ALU.max))
                seq(V.tensor_tensor(eq, src, wide(top_w[:, k, :]), ALU.is_equal))
                seq(V.tensor_tensor(key, eq, desc, ALU.mult))
                seq(V.tensor_reduce(best, key, AX.X, ALU.max))
                seq(V.tensor_tensor(oh, key, wide(best), ALU.is_equal))
                if k == 0:
                    seq(V.scalar_tensor_tensor(out=S2, in0=oh1, scalar=-4.0, in1=S, op0=ALU.mult, op1=ALU.add))
            V.tensor_tensor(mask.rearrange("p (t e) -> p t e", e=E), oh1, oh2, ALU.add).then_inc(mask_ok, 1)
            dve.wait_ge(rank_ps, 1)
            in_tile = ps_log[:, 0:256].rearrange("p (t e) -> p t e", e=E)
            total = ps_log[:, 256:512].rearrange("p (t e) -> p t e", e=E)
            for e in range(E):
                own.mark(V.tensor_tensor_scan(cum[:, :, e], one, total[:, :, e], 0.0, ALU.mult, ALU.add))
            own.settle()
            own.mark(V.tensor_scalar(count_i, cum[:, TILES - 1, :], float(ROWS - 1), None, ALU.add))
            seq(V.tensor_tensor(tmp, cum, total, ALU.subtract))
            seq(V.tensor_tensor(rank, tmp, in_tile, ALU.add))
            seq(V.tensor_scalar(pad_i, count_i, -ROWS, None, ALU.bitwise_and))
            seq(V.tensor_copy(pad, pad_i))
            seq(V.tensor_tensor_scan(pad_end, one[:, 0:E], pad, 0.0, ALU.mult, ALU.add))
            seq(V.tensor_tensor(base, pad_end, pad, ALU.subtract))
            seq(V.tensor_tensor(pos, rank, base.unsqueeze(1).to_broadcast([P, TILES, E]), ALU.add))
            for k, oh in enumerate((oh1, oh2)):
                seq(V.tensor_tensor(tmp, oh, pos, ALU.mult))
                seq(V.tensor_reduce(row1, tmp, AX.X, ALU.add))
                own.mark(V.tensor_copy(y_row[:, k, :], row1))
                seq(V.tensor_copy(row_i, row1))
                own.mark(V.tensor_scalar(row_lo, row_i, P - 1, None, ALU.bitwise_and))
                seq(V.tensor_scalar(row_hi, row_i, 7, None, ALU.arith_shift_right))
                seq(V.scalar_tensor_tensor(out=l_row[:, k, :], in0=row_lo, scalar=float(QR), in1=row_hi,
                                           op0=ALU.mult, op1=ALU.add))
            seq(V.tensor_tensor(cmp_, pad_end.unsqueeze(1).to_broadcast([P, ROUTED, E]),
                                starts.unsqueeze(2).to_broadcast([P, ROUTED, E]), ALU.is_le))
            seq(V.tensor_reduce(sets, cmp_, AX.X, ALU.add))
            seq(V.tensor_scalar(slot_set[:, LEAD:LEAD + ROUTED], sets, float(E - 1), 1.0, ALU.min, ALU.add))
            V.engine_nop().then_inc(route_ok, 1)

            V.engine_nop().then_inc(hhl_ok, RING)
            V.engine_nop().then_inc(y_ok, 2)

            def parameters(n, u):
                s = dve.value_load(slot_set[0:1, bass.ds(n, 1)], min_val=0, max_val=NW - 1)
                V.tensor_copy(par[u][:, :], PT[:, bass.ds(s, 1), :].squeeze(1)).then_inc(par_ok, 1)

            def rows_T(n, u):
                dve.wait_ge(rowsT_ps, n + 1)
                V.tensor_copy(xgT[u][:, :, :].bitcast(I32), ps_s.bitcast(I32)).then_inc(rowsT_ok, 1)

            def split_h(n, j, u):
                dve.wait_ge(gelu_ok, n * KH + j + 1 + RING)
                dve.wait_ge(y_ps, n * KH + j + 1)
                own.mark(V.tensor_scalar(hhl[j % RING][:, 0, :], h32[j % RING], par[u][:, 1:2], None, ALU.mult))
                own.settle()
                V.scalar_tensor_tensor(out=hhl[j % RING][:, 1, :], in0=h32[j % RING], scalar=par[u][:, 1:2],
                                       in1=hhl[j % RING][:, 0, :], op0=ALU.mult,
                                       op1=ALU.subtract).then_inc(hhl_ok, 1)

            def result(n, u):
                dve.wait_ge(y_ps, (n + 1) * KH + RING)
                dve.wait_ge(y_out[u], (n - u) * 8)
                for t in range(2):
                    ins = V.scalar_tensor_tensor(out=y_sb[u][:, t * D:(t + 1) * D], in0=ps_y[u][:, t * D:(t + 1) * D],
                                                 scalar=par[u][:, 2:3], in1=par[u][:, PAR:PAR + D],
                                                 op0=ALU.mult, op1=ALU.add)
                ins.then_inc(y_ok, 1)

            def slot(n, u, first=False, final=False):
                split_h(n, 0, u)
                if not first:
                    result(n - 1, 1 - u)
                for j in range(1, 4):
                    split_h(n, j, u)
                if not final:
                    rows_T(n + 1, 1 - u)
                    parameters(n + 1, 1 - u)
                for j in range(4, KH):
                    split_h(n, j, u)

            def add_up(m, u):
                dve.wait_ge(fin_in[u], (m - u) * 48 + 96)
                seq(V.tensor_tensor(racc[u], racc[u], ysh[u], ALU.add))
                for t in range(2):
                    acc = racc[u][:, t * D:(t + 1) * D]
                    for k in range(2):
                        ins = V.scalar_tensor_tensor(out=acc, in0=yg[u][:, t, k, :],
                                                     scalar=top_w[:, k, bass.ds(m * 2 + t, 1)],
                                                     in1=acc, op0=ALU.mult, op1=ALU.add)
                        if (t, k) == (1, 1):
                            ins.then_inc(fin_ok, 1)
                        else:
                            seq(ins)

            rows_T(0, 0)
            parameters(0, 0)
            slot(0, 0, first=True)
            slot(1, 1)
            slot(2, 0)
            with own.loop((LEAD + ROUTED - 3) // 2, 2 * KH) as it:
                for v in range(2):
                    slot(it * 2 + 3 + v, (3 + v) % 2)
            with own.loop(TRAIL // 2 - 1, 2 * (KH + 8)) as it:
                for v in range(2):
                    slot(it * 2 + LEAD + ROUTED + v, (LEAD + ROUTED + v) % 2)
                    for w in range(2):
                        add_up((it * 2 + v) * 2 + w, w)
            for v in range(2):
                n = SLOTS - 2 + v
                slot(n, n % 2, final=v == 1)
                if v == 1:
                    result(n, n % 2)
                for w in range(2):
                    add_up((TRAIL - 2 + v) * 2 + w, w)

        @block.tensor
        def _(pe):
            T = nc.tensor

            def x_transposes(b):
                pe.wait_ge(xhl_ok, b + 1)
                for i in range(2):
                    for q in range(2):
                        for t in range(TPB):
                            c = (2 * i + q) * P
                            ins = T.transpose(ps_xT[i][:, q * SEQ + t * P:q * SEQ + (t + 1) * P],
                                              xhl[:, t, c:c + P], ident[:, :])
                ins.then_inc(xT_ps, 1)

            PASSES = ((0, 0), (0, 1), (1, 0))

            def logits(b):
                pe.wait_ge(xT_ok, b + 1)
                for t in range(TPB):
                    n = 0
                    for c in range(KD):
                        for xp, wp in PASSES:
                            ins = T.matmul(ps_log[:, bass.ds((b * TPB + t) * E, E)],
                                           xTA[:, 2 * xp + c, t * P:(t + 1) * P],
                                           gw[:, wp, c, GATES:GCOL], start=n == 0, stop=n == 5)
                            n += 1
                ins.then_inc(logit_ok, 1)

            def projections(b):
                for ch in range(KD):
                    for g in range(3):
                        pe.wait_ge(proj_act, b * 6 + 3 * ch + g + 1)
                        n = 0
                        for c in range(KD):
                            for xp, wp in PASSES:
                                o = g * D + ch * P
                                ins = T.matmul(ps_g[g][:, :], gw[:, wp, c, o:o + P], xTA[:, 2 * xp + c, :],
                                               start=n == 0, stop=n == 5)
                                n += 1
                        ins.then_inc(proj_ps, 1)

            def scan_transposes(b):
                pe.wait_ge(r_ok, b + 1)
                for ch in range(KD):
                    pe.wait_ge(scan_ok, b * 2 + ch + 1 + 2)
                    for t in range(TPB):
                        o = (t % 2) * D + ch * P
                        ins = T.transpose(ps_r[t // 2][:, o:o + P], tv[ch][:, t * P:(t + 1) * P], identf[:, :])
                    ins.then_inc(scanT_ps, 1)

            pe.nop().then_inc(scanT_ps, 2)
            pe.nop().then_inc(y_ps, RING)
            pe.wait_ge(const_ok, 4)
            x_transposes(0)
            pe.wait_ge(stage_used[0], 1)
            logits(0)
            with pe.Fori(0, SEQS - 1) as b:
                projections(b)
                x_transposes(b + 1)
                logits(b + 1)
                scan_transposes(b)
            projections(SEQS - 1)
            scan_transposes(SEQS - 1)

            pe.wait_ge(mask_ok, 1)
            T.matmul(ps_log[:, 0:256], before[:, :], mask, start=True, stop=True)
            T.matmul(ps_log[:, 256:512], ones[:, :], mask, start=True, stop=True).then_inc(rank_ps, 1)

            def row_transposes(n, u):
                pe.wait_ge(rows_in[u], (n - u) * 16 + 32)
                pe.wait_ge(rowsT_ok, n)
                for q in range(4):
                    for t in range(2):
                        ins = T.transpose(ps_s[:, q, t * P:(t + 1) * P], xg[u][:, t, q * P:(q + 1) * P], ident[:, :])
                ins.then_inc(rowsT_ps, 1)

            def weight_set(n):
                s = pe.value_load(slot_set[0:1, bass.ds(n, 1)], min_val=0, max_val=NW - 1)
                return pe.snap(s * WSET)

            def layer1(n, j, u, w):
                pe.wait_ge(gelu_ok, n * KH + j + 1)
                i = 0
                for c in range(KD):
                    for wp in range(2):
                        for xp in range(2 - wp):
                            ins = T.matmul(ps_h[j % RING][:, 0:ROWS],
                                           W[:, bass.ds(w + wp * HALF + c * H + j * P, P)],
                                           xgT[u][:, 2 * xp + c, :], start=i == 0, stop=i == 5)
                            i += 1
                ins.then_inc(h_ps, 1)

            def layer2(n, j, u, w):
                pe.wait_ge(hhl_ok, n * KH + j + 1 + RING)
                if j == 0:
                    pe.wait_ge(y_ok, n + 1)
                for t in range(2):
                    for hp, wp in PASSES:
                        ins = T.matmul(ps_y[u][:, t * D:(t + 1) * D], hhl[j % RING][:, hp, t * P:(t + 1) * P],
                                       W[:, bass.ds(w + (2 + wp) * HALF + j * D, D)],
                                       start=(j, t, hp, wp) == (0, 0, 0, 0), stop=(j, hp, wp) == (KH - 1, 1, 0),
                                       skip_group_check=True)
                ins.then_inc(y_ps, 1)

            def slot(n, u, w, final=False):
                w_next = None
                for j in range(KH):
                    if j + AHEAD < KH:
                        layer1(n, j + AHEAD, u, w)
                    elif not final:
                        if w_next is None:
                            pe.wait_ge(rowsT_ok, n + 2)
                            w_next = weight_set(n + 1)
                        layer1(n + 1, j + AHEAD - KH, 1 - u, w_next)
                    layer2(n, j, u, w)
                    if j == 1 and not final:
                        row_transposes(n + 1, 1 - u)

            pe.wait_ge(route_ok, 1)
            row_transposes(0, 0)
            pe.wait_ge(rowsT_ok, 1)
            w0 = weight_set(0)
            for j in range(AHEAD):
                layer1(0, j, 0, w0)
            with pe.Fori(0, SLOTS // 2) as it:
                for u in range(2):
                    slot(it * 2 + u, u, weight_set(it * 2 + u))
            slot(SLOTS - 1, 0, weight_set(SLOTS - 1), final=True)


def kernel(**inputs):
    import numpy as np
    import concourse.bacc as bacc
    from concourse.bass_utils import run_bass_kernel_spmd

    a = {k.replace("L0_", ""): np.asarray(v) for k, v in inputs.items()}
    b1 = np.concatenate([a["ffn_bs1"][None], a["ffn_b1"]])
    arrays = {
        "x": a["attn_x"].reshape(TOKENS, D),
        "w1": np.concatenate([a["ffn_Ws1"][None], a["ffn_W1"]]).transpose(0, 2, 1),
        "w2": np.concatenate([a["ffn_Ws2"][None], a["ffn_W2"]]).transpose(0, 2, 1),
        "gates": np.concatenate([a["attn_Wg"], a["attn_Wv"], a["attn_Wd"], a["ffn_Wg"].T], axis=1),
        "b1": b1.reshape(NW, KH, P).transpose(2, 0, 1),
        "b2": np.concatenate([a["ffn_bs2"][None], a["ffn_b2"]]),
        "gbias": np.stack([a["ffn_bg"], a["ffn_bias"]]),
        "sbias": np.stack([a["attn_bg"], a["attn_bv"], a["attn_bd"]]).reshape(3 * KD, P).T,
    }
    arrays = {f"in_{k}": np.ascontiguousarray(v) for k, v in arrays.items()}
    nc = bacc.Bacc("TRN2", target_bir_lowering=False, num_devices=1)
    aps = [nc.dram_tensor(k, v.shape, mybir.dt.from_np(v.dtype), kind="ExternalInput").ap() for k, v in arrays.items()]
    out = nc.dram_tensor("out", (TOKENS, D), F32, kind="ExternalOutput").ap()
    layer(nc, *aps, out)
    r = run_bass_kernel_spmd(nc, [arrays], core_ids=[0])
    return r.results[0]["out"].reshape(SEQS, SEQ, D)
```

```python
from contextlib import ExitStack, contextmanager

import concourse.bass as bass
from concourse import mybir

F32, F16, I32, U32 = mybir.dt.float32, mybir.dt.float16, mybir.dt.int32, mybir.dt.uint32
ALU, ACT, AX = mybir.AluOpType, mybir.ActivationFunctionType, mybir.AxisListType
RMAX, RADD = bass.bass_isa.ReduceOp.max, bass.bass_isa.ReduceOp.add

P = 128
SEQS, SEQ, D, H, E = 8, 512, 256, 1024, 8
TOKENS = SEQS * SEQ
TPB = SEQ // P
KD, KH = D // P, H // P
ROWS = 256
SLOTS = 2 * TOKENS // ROWS + E - 1
LIST = E * TOKENS + (E - 1) * ROWS
NW = E + 1
HALF = KD * H
WSET = 4 * HALF
GATES = 3 * D
GCOL = GATES + E
XSCALE = 256.0
TOP = 2.0 ** 14
EXPONENT = 0x7F800000
EPS = 1e-5
SATURATED = 17.5
RING = 4
AHEAD = 3
PROJ = 6
EVENTS = PROJ + 2 * KH
EV_A, H_A, S_A = SEQS * EVENTS, SEQS * 2 * KH, 2 * SEQS
PER = 54
NPAR = 12


class Tally:

    def __init__(self, eng, sem):
        self.eng, self.sem, self.base, self.k = eng, sem, 0, 0

    def mark(self, ins):
        ins.then_inc(self.sem, 1)
        self.k += 1

    def settle(self):
        self.eng.wait_ge(self.sem, self.base + self.k)

    @contextmanager
    def loop(self, trips, per):
        start = self.k
        assert not self.base
        with self.eng.Fori(0, trips) as i:
            self.base, self.k = i * per + start, 0
            yield i
            assert self.k == per, self.k
        self.base, self.k = 0, start + trips * per


def layer(nc, x, w1, w2, gates, b1, b2, gbias, sbias, out):
    ctx = ExitStack()
    with ctx:
        def sb(name, shape, dt):
            return ctx.enter_context(nc.sbuf_tensor(name, shape, dt))

        def sem(name):
            return ctx.enter_context(nc.semaphore(name))

        xhl_dram = nc.dram_tensor("xhl_rows", (TOKENS + ROWS, 2 * D), F16, kind="Internal").ap()
        list_dram = nc.dram_tensor("lists", (LIST, 2), U32, kind="Internal").ap()

        W = sb("W", [P, NW * WSET], F16)
        PT = sb("PT", [P, NW, NPAR], F32)
        par = [sb(f"par{i}", [P, NPAR], F32) for i in range(2)]
        b2row = [sb(f"b2row{i}", [P, D], F32) for i in range(2)]
        stage = [sb(f"stage{i}", [P, HALF], F32) for i in range(2)]
        rows = [sb(f"rows{i}", [P, 4 * SEQ], F16) for i in range(2)]
        arena = sb("arena", [P, 7680], F32)
        small = sb("small", [P, 256], F32)
        rt = sb("rt", [P, 480], F32)
        bs2 = sb("bs2", [P, D], F32)
        ident = sb("ident", [P, P], F16)
        identf = sb("identf", [P, P], F32)
        before = sb("before", [P, P], F16)
        ones = sb("ones", [P, P], F16)
        token = sb("token", [P, SEQS * TPB], U32)
        entry = [sb(f"entry{i}", [P, 4 * TPB], U32) for i in range(2)]
        place = [sb(f"place{i}", [P, 2 * TPB], U32) for i in range(2)]
        slot_list = [sb(f"slot_list{i}", [P, 2, 2], U32) for i in range(2)]
        slot_add = [sb(f"slot_add{i}", [P, 2, 2], U32) for i in range(2)]
        slot_set = sb("slot_set", [P, SLOTS], I32)
        slot_at = sb("slot_at", [P, SLOTS], I32)

        xT = [r[:, :].rearrange("p (q n) -> p q n", q=4) for r in rows]
        xg = [rows[0][:, i * 1024:(i + 1) * 1024].rearrange("p (t n) -> p t n", t=2) for i in range(2)]
        xgT = [rows[1][:, i * 1024:(i + 1) * 1024].rearrange("p (q n) -> p q n", q=4) for i in range(2)]
        h32 = [arena[:, i * ROWS:(i + 1) * ROWS] for i in range(RING)]
        hhl = [arena[:, 1024 + i * ROWS:1024 + (i + 1) * ROWS].bitcast(F16).rearrange(
            "p (s n) -> p s n", s=2) for i in range(RING)]
        xt = [arena[:, 2048 + i * 1024:3072 + i * 1024] for i in range(2)]
        acc = arena[:, 4096:5120]
        sg = [arena[:, 5120 + i * 512:5632 + i * 512] for i in range(2)]
        tv = [arena[:, 6144 + i * 512:6656 + i * 512] for i in range(2)]
        dec = arena[:, 7168:7680]
        graw = arena[:, 4096:4096 + KD * GCOL]
        spare = arena[:, 6144:6656].bitcast(U32)
        zeros = arena[:, 6656:7168]
        y_sb = [arena[:, 2048 + i * 512:2560 + i * 512] for i in range(2)]
        last = (NW - 1) * WSET
        gw_flat = W[:, last:last + 2 * KD * GCOL].rearrange("p (s n) -> p s n", s=2)
        gw = W[:, last:last + 2 * KD * GCOL].rearrange("p (s c n) -> p s c n", s=2, c=KD)
        at = last + 2 * KD * GCOL
        xhl = W[:, at:at + 4 * SEQ].rearrange("p (t n) -> p t n", t=TPB)
        xs = W[:, at + 4 * SEQ:at + 8 * SEQ].bitcast(F32)
        assert at + 8 * SEQ <= NW * WSET

        stats = small[:, 0:24].rearrange("p (t n) -> p t n", t=TPB)
        mv = small[:, 24:32].rearrange("p (t n) -> p t n", t=TPB)
        ve, rs, neghalf, half = small[:, 32:36], small[:, 36:40], small[:, 40:44], small[:, 44:46]
        ssq, ssum, norm = small[:, 46:48], small[:, 48:50], small[:, 50:53]
        pw, ip, scl, inv = small[:, 56:59], small[:, 60:63], small[:, 64:67], small[:, 68:71]
        a_gate, a_half = small[:, 72:73], small[:, 73:74]
        b1max, b1red = small[:, 80:89], small[:, 90:99]
        gb, gb2 = small[:, 100:108], small[:, 108:116]
        sbt = small[:, 116:122]
        count = small[:, 124:132]
        count_i, pad_i = small[:, 132:140].bitcast(I32), small[:, 140:148].bitcast(I32)
        pad, pad_end, room = small[:, 148:156], small[:, 156:164], small[:, 164:172]
        scratch = small[:, 172:173]
        carry, ebase = small[:, 176:184], small[:, 184:192]
        one = small[:, 192:200]
        top_z = small[:, 200:208].rearrange("p (k t) -> p k t", k=2)
        top_t = small[:, 208:216]
        best = small[:, 216:220]
        place_f = small[:, 220:228]
        scratch_a, scratch_p = small[:, 228:229], small[:, 230:232]

        def table(a, b):
            return rt[:, a:b].rearrange("p (t e) -> p t e", e=E)

        z, eq, key, z2, pos, desc = (table(i * 32, i * 32 + 32) for i in range(6))
        oh = rt[:, 192:256].rearrange("p (k t e) -> p k t e", k=2, e=E)
        ohp = rt[:, 256:320].rearrange("p (k t e) -> p k t e", k=2, e=E)
        mask = rt[:, 320:336].bitcast(F16)
        starts, starts_i = rt[:, 340:340 + SLOTS], rt[:, 380:380 + SLOTS].bitcast(I32)
        sets = rt[:, 420:420 + SLOTS]
        ended = arena[:, 2048:2048 + SLOTS * E].rearrange("p (i e) -> p i e", e=E)
        moved = arena[:, 2560:2560 + SLOTS * E].rearrange("p (i e) -> p i e", e=E)

        bank = [ctx.enter_context(nc.psum_tensor(f"bank{i}", [P, 512], F32)) for i in range(8)]
        ps_e = bank[0:4]
        ps_y = bank[4:6]
        ps_t = bank[6]
        ps_t16 = ps_t[:, :].bitcast(F16)
        ps_l = bank[7]

        x_in = [sem(f"x_in{i}") for i in range(2)]
        w_in = [sem(f"w_in{i}") for i in range(2)]
        gate_in, tab_in, bs2_in = sem("gate_in"), sem("tab_in"), sem("bs2_in")
        const_ok = sem("const_ok")
        spare_ok = sem("spare_ok")
        spare_out = sem("spare_out")
        stage_used = [sem(f"stage_used{i}") for i in range(2)]
        gw_ok = sem("gw_ok")
        ssq_ok, norm_ok, scale_ok, whi_ok = sem("ssq_ok"), sem("norm_ok"), sem("scale_ok"), sem("whi_ok")
        var_ok, rs_ok, xs_ok, xhi_ok, xhl_ok = (sem(n) for n in ("var_ok", "rs_ok", "xs_ok", "xhi_ok", "xhl_ok"))
        bias_ok = sem("bias_ok")
        b1_ok, iota_ok, bias_half = sem("b1_ok"), sem("iota_ok"), sem("bias_half")
        xhl_out = sem("xhl_out")
        xT_ps, xT_ok = sem("xT_ps"), sem("xT_ok")
        logit_ps, top_ok, tanh_ok, mask_ok, rank_ps = (
            sem(n) for n in ("logit_ps", "top_ok", "tanh_ok", "mask_ok", "rank_ps"))
        place_ok, entry_ok = sem("place_ok"), sem("entry_ok")
        list_out = [sem(f"list_out{i}") for i in range(2)]
        ev_ps, ev_act = sem("ev_ps"), sem("ev_act")
        hhl_ok, y_ps, y_ok = sem("hhl_ok"), sem("y_ps"), sem("y_ok")
        scan_ok, scanT_ps, r_ok = sem("scan_ok"), sem("scanT_ps"), sem("r_ok")
        o_out = sem("o_out")
        route_ok = sem("route_ok")
        list_in = [sem(f"list_in{i}") for i in range(2)]
        b2_in = [sem(f"b2_in{i}") for i in range(2)]
        rows_in = [sem(f"rows_in{i}") for i in range(2)]
        rowsT_ps, rowsT_ok, par_ok = sem("rowsT_ps"), sem("rowsT_ok"), sem("par_ok")
        add_out = [sem(f"add_out{i}") for i in range(2)]
        dve_own, pool_own = sem("dve_own"), sem("pool_own")

        block = ctx.enter_context(nc.Block())

        x_v = x.rearrange("(b t p) d -> b p t d", t=TPB, p=P)
        xhl_v = xhl_dram[0:TOKENS].rearrange("(b t p) d -> b p t d", t=TPB, p=P)
        out_v = out[0:TOKENS].rearrange("(b t p) d -> b p t d", t=TPB, p=P)
        w1_v = w1.rearrange("e (c p) h -> e p c h", p=P)
        w2_v = w2.rearrange("e (j p) d -> e p j d", p=P)

        def chunks(ap, n):
            return ap.rearrange("p (t n) -> p t n", t=n)

        @block.sync
        def _(sp):
            def load_x(b):
                sp.dma_start(chunks(xt[b % 2], TPB), x_v[b]).then_inc(x_in[b % 2], 16)

            def load_w(layer_, n):
                sp.dma_start(chunks(stage[layer_][:, :], (KD, KH)[layer_]),
                             (w1_v, w2_v)[layer_][n]).then_inc(w_in[layer_], 16)

            load_x(0)
            sp.dma_start(chunks(graw, KD), gates.rearrange("(c p) n -> p c n", p=P)).then_inc(gate_in, 16)
            load_w(0, 0)
            load_w(1, 0)
            sp.dma_start(PT[:, :, 4:NPAR], b1).then_inc(tab_in, 16)
            sp.dma_start(gb, gbias[0].partition_broadcast(P)).then_inc(tab_in, 16)
            sp.dma_start(gb2, gbias[1].partition_broadcast(P)).then_inc(tab_in, 16)
            sp.dma_start(sbt, sbias).then_inc(tab_in, 16)
            sp.dma_start(bs2[:, :], b2[0].partition_broadcast(P)).then_inc(bs2_in, 16)
            load_x(1)
            sp.wait_ge(spare_ok, 2)
            list_v = list_dram.rearrange("(b r) c -> b (r c)", r=ROWS)
            sp.dma_start(list_v[0:P], spare).then_inc(spare_out, 16)
            sp.dma_start(list_v[P:LIST // ROWS], spare[0:LIST // ROWS - P]).then_inc(spare_out, 16)
            sp.dma_start(xhl_dram[TOKENS:].rearrange("(p t) d -> p (t d)", t=2),
                         zeros.bitcast(F16)).then_inc(spare_out, 16)
            sp.dma_start(out[TOKENS:].rearrange("(p t) d -> p (t d)", t=2), zeros).then_inc(spare_out, 16)

            def store_xhl(b):
                sp.wait_ge(xhl_ok, b + 1)
                sp.dma_start(xhl_v[b], xhl).then_inc(xhl_out, 16)

            def store_base(b):
                sp.wait_ge(y_ok, 2 * b + 2 + 2)
                sp.dma_start(out_v[b], chunks(acc, TPB)).then_inc(o_out, 16)

            def next_weights(n):
                for l in range(2):
                    sp.wait_ge(stage_used[l], n)
                    load_w(l, n)

            next_weights(1)
            store_xhl(0)
            for b in range(SEQS):
                if b:
                    store_base(b - 1)
                if b + 2 < NW:
                    next_weights(b + 2)
                if b + 2 < SEQS:
                    sp.wait_ge(r_ok, 2 * b + 2)
                    load_x(b + 2)
                if b + 1 < SEQS:
                    store_xhl(b + 1)
                if b == SEQS - 1:
                    sp.wait_ge(route_ok, 1)
                    for u in range(2):
                        sp.wait_ge(list_out[u], SEQS // 2 * 2 * TPB * 16)
                    sp.wait_ge(spare_out, 64)

                    def look_up(n):
                        return (sp.value_load(slot_at[0:1, bass.ds(n, 1)], min_val=0, max_val=LIST - ROWS),
                                sp.value_load(slot_set[0:1, bass.ds(n, 1)], min_val=0, max_val=NW - 1))

                    def entries(a, u):
                        sp.dma_start(slot_list[u][:, :, :], list_dram[bass.ds(a, ROWS), :].rearrange(
                            "(p t) c -> p t c", t=2)).then_inc(list_in[u], 16)

                    def second_bias(s, u):
                        sp.dma_start(b2row[u][:, :].unsqueeze(1),
                                     b2[bass.ds(s, 1), :].partition_broadcast(P)).then_inc(b2_in[u], 16)

                    for u in range(2):
                        a, s = look_up(u)
                        entries(a, u)
                        second_bias(s, u)
                    store_base(b)

            def slot(n, u):
                a, s = look_up(n)
                sp.wait_ge(rowsT_ps, n - 1)
                sp.wait_ge(par_ok, n - 1)
                entries(a, u)
                sp.wait_ge(y_ok, S_A + n - 1 + 2)
                second_bias(s, u)

            with sp.Fori(0, (SLOTS - 3) // 2) as it:
                for u in range(2):
                    slot(it * 2 + 2 + u, u)
            slot(SLOTS - 1, 0)
            sp.wait_ge(o_out, 16 * SEQS)

        @block.gpsimd
        def _(pool):
            own = Tally(pool, pool_own)

            def made(ins):
                own.mark(ins)

            made(pool.memset(neghalf, -0.5))
            made(pool.memset(half, 0.5))
            made(pool.memset(ident[:, :], 0.0))
            made(pool.memset(identf[:, :], 0.0))
            made(pool.memset(before[:, :], 0.0))
            pool.memset(ones[:, :], 1.0).then_inc(const_ok, 1)
            own.settle()
            for m in (ident, identf):
                pool.affine_select(out=m[:, :], in_=m[:, :], compare_op=ALU.not_equal, fill=1.0, base=0,
                                   pattern=[[-1, P]], channel_multiplier=1).then_inc(const_ok, 1)
            pool.affine_select(out=before[:, :], in_=before[:, :], compare_op=ALU.is_ge, fill=1.0, base=0,
                               pattern=[[-1, P]], channel_multiplier=1).then_inc(const_ok, 1)

            def rstd(b):
                pool.wait_ge(var_ok, b + 1)
                pool.tensor_tensor(out=rs, in0=ve, in1=neghalf, op=ALU.pow).then_inc(rs_ok, 1)

            def norms(n):
                pool.wait_ge(ssq_ok, n + 1)
                made(pool.partition_all_reduce(ssum, ssq, P, RADD))
                own.settle()
                pool.tensor_tensor(out=norm[:, 0:2], in0=ssum, in1=half, op=ALU.pow).then_inc(norm_ok, 1)

            def low_second(n):
                o = n * WSET + 2 * HALF
                pool.wait_ge(whi_ok, 2 * n + 3)
                made(pool.tensor_scalar(stage[1][:, :], stage[1][:, :], scl[:, 1:2], None, ALU.mult))
                own.settle()
                pool.tensor_tensor(out=W[:, o + HALF:o + 2 * HALF], in0=stage[1][:, :], in1=W[:, o:o + HALF],
                                   op=ALU.subtract).then_inc(stage_used[1], 1)

            def x_low(b):
                pool.wait_ge(xhi_ok, b + 1)
                pool.tensor_tensor(out=xhl[:, :, D:2 * D], in0=chunks(xs, TPB), in1=xhl[:, :, 0:D],
                                   op=ALU.subtract).then_inc(xhl_ok, 1)

            def add_bias(b):
                v = chunks(xt[b % 2], TPB)
                pool.tensor_tensor(out=v, in0=v, in1=bs2[:, :].unsqueeze(1).to_broadcast([P, TPB, D]),
                                   op=ALU.add).then_inc(bias_ok, 1)

            def fill_entries(b):
                u = b % 2
                if b >= 2:
                    pool.wait_ge(list_out[u], b // 2 * 2 * TPB * 16)
                for k in range(2):
                    v = entry[u][:, :].rearrange("p (k t c) -> p k t c", k=2, c=2)[:, k, :, 0]
                    pool.tensor_copy(v, token[:, b * TPB:(b + 1) * TPB]).then_inc(entry_ok, 1)

            def scatter(b):
                u = b % 2
                pool.wait_ge(entry_ok, 2 * b + 2)
                pool.wait_ge(place_ok, b + 1)
                for c in range(2 * TPB):
                    pool.indirect_dma_start(
                        list_dram, bass.IndirectOffsetOnAxis(ap=place[u][:, c:c + 1], axis=0),
                        entry[u][:, 2 * c:2 * c + 2], None).then_inc(list_out[u], 16)

            rstd(0)
            norms(0)
            made(pool.iota(spare.rearrange("p (r c) -> p r c", c=2)[:, :, 0], pattern=[[1, ROWS]], base=TOKENS,
                           channel_multiplier=0))
            pool.memset(spare.rearrange("p (r c) -> p r c", c=2)[:, :, 1], 0).then_inc(spare_ok, 1)
            pool.memset(zeros, 0.0).then_inc(spare_ok, 1)
            made(pool.iota(token[:, :], pattern=[[P, SEQS * TPB]], base=0, channel_multiplier=1))
            made(pool.iota(starts_i, pattern=[[ROWS, SLOTS]], base=0, channel_multiplier=0))
            own.settle()
            pool.nop().then_inc(iota_ok, 1)
            fill_entries(0)
            x_low(0)
            pool.wait_ge(b1_ok, 1)
            made(pool.partition_all_reduce(b1red, b1max, P, RMAX))
            own.settle()
            norms(1)
            low_second(0)
            pool.wait_ge(bs2_in, 16)
            add_bias(0)
            pool.wait_ge(spare_out, 64)
            for b in range(SEQS):
                if b + 2 < NW:
                    norms(b + 2)
                if b + 1 < SEQS:
                    rstd(b + 1)
                    x_low(b + 1)
                    add_bias(b + 1)
                    low_second(b + 1)
                scatter(b)
                if b + 1 < SEQS:
                    fill_entries(b + 1)
                if b + 1 == SEQS:
                    norms(NW)
                    low_second(NW - 1)

            def hold():
                own.settle()
                made(pool.tensor_tensor(out=scratch_p, in0=half, in1=half, op=ALU.mult))

            def gather(n, u, wait=True):
                if wait:
                    pool.wait_ge(rowsT_ps, n - 1)
                pool.wait_ge(list_in[u], (n - u) * 8 + 16)
                if wait:
                    hold()
                for t in range(2):
                    pool.indirect_dma_start(
                        xg[u][:, t, :], None, xhl_dram,
                        bass.IndirectOffsetOnAxis(ap=slot_list[u][:, t, 0:1], axis=0)).then_inc(rows_in[u], 16)

            def scatter_add(n, u, wait=True):
                pool.wait_ge(y_ok, S_A + n + 1 + 2)
                if wait:
                    pool.wait_ge(add_out[1 - u], (n + u) * 16)
                hold()
                for t in range(2):
                    pool.indirect_dma_start(
                        out, bass.IndirectOffsetOnAxis(ap=slot_add[u][:, t, 0:1], axis=0),
                        y_sb[u][:, t * D:(t + 1) * D], None, compute_op=ALU.add).then_inc(add_out[u], 16)

            pool.wait_ge(xhl_out, 16 * SEQS)
            pool.wait_ge(ev_ps, EVENTS * (SEQS - 1))
            gather(0, 0, wait=False)
            gather(1, 1, wait=False)
            pool.wait_ge(o_out, 16 * SEQS)
            for u in range(2):
                gather(2 + u, u)
                scatter_add(u, u, wait=u > 0)
            with own.loop((SLOTS - 5) // 2, 4) as it:
                for u in range(2):
                    gather(it * 2 + 4 + u, u)
                    scatter_add(it * 2 + 2 + u, u)
            gather(SLOTS - 1, 0)
            for n in range(SLOTS - 3, SLOTS):
                scatter_add(n, n % 2)
            for u in range(2):
                pool.wait_ge(add_out[u], 32 * ((SLOTS + 1 - u) // 2))

        @block.scalar
        def _(act):
            A = nc.scalar.activation

            def squares(n, l):
                act.wait_ge(w_in[l], (n + 1) * 16)
                act.wait_ge(norm_ok, n + 1)
                o = n * WSET + l * 2 * HALF
                ins = A(W[:, bass.ds(o, HALF)], stage[l][:, :], ACT.Square, accum_out=ssq[:, l:l + 1])
                if l:
                    ins.then_inc(ssq_ok, 1)

            def high_part(n, l):
                if l == 0:
                    act.wait_ge(scale_ok, n + 2)
                    A(scratch_a, half[:, 0:1], ACT.Copy)
                o = n * WSET + l * 2 * HALF
                A(W[:, bass.ds(o, HALF)], stage[l][:, :], ACT.Copy, scale=scl[:, l:l + 1]).then_inc(whi_ok, 1)

            def x_high(b):
                act.wait_ge(xs_ok, b + 1)
                A(xhl[:, :, 0:D], chunks(xs, TPB), ACT.Copy).then_inc(xhi_ok, 1)

            def x_T(b, u, i):
                act.wait_ge(xT_ps, b * 2 + i + 1)
                A(xT[u][:, 2 * i:2 * i + 2, :], chunks(ps_t16, 2), ACT.Copy).then_inc(xT_ok, 1)

            def score(b):
                act.wait_ge(top_ok, b + 1)
                A(top_t, small[:, 200:208], ACT.Tanh, scale=0.5).then_inc(tanh_ok, 1)

            def projection(b, u, i):
                ch, g = divmod(i, 3)
                act.wait_ge(ev_ps, b * EVENTS + i + 1)
                if g == 0:
                    act.wait_ge(scanT_ps, b * 2 + 2)
                if i == 5:
                    act.wait_ge(scan_ok, b * 2 + 1)
                A((sg[ch], tv[ch], dec)[g], ps_e[(2 * u + i) % RING][:, :], ACT.Tanh,
                  bias=sbt[:, 2 * g + ch:2 * g + ch + 1], scale=(a_half, a_gate, a_half)[g]).then_inc(ev_act, 1)

            def gelu(ev, m, i, k, p):
                act.wait_ge(ev_ps, ev + 1)
                act.wait_ge(hhl_ok, m + 1)
                A(h32[i % RING], ps_e[k % RING][:, 0:ROWS], ACT.Gelu, bias=p[:, 4 + i % KH:5 + i % KH],
                  scale=p[:, 0:1]).then_inc(ev_act, 1)

            def sequence(b, u, last_=False):
                for i in range(3):
                    projection(b, u, i)
                if not last_:
                    high_part(b + 1, 0)
                for i in range(3, PROJ):
                    projection(b, u, i)
                if not last_:
                    act.wait_ge(xhl_out, b * 16 + 16)
                    x_high(b + 1)
                    high_part(b + 1, 1)
                else:
                    act.wait_ge(xhl_out, 16 * SEQS)
                    squares(NW - 1, 0)
                    squares(NW - 1, 1)
                for i in range(2 * KH):
                    gelu(b * EVENTS + PROJ + i, b * 2 * KH + i, i, 2 * u + PROJ + i, PT[:, 0, :])
                    if not last_:
                        if i in (9, 11):
                            x_T(b + 1, 1 - u, (i - 9) // 2)
                        if i in (12, 14) and more_weights:
                            squares(b + 2, (i - 12) // 2)
                    elif i in (5, 7):
                        high_part(NW - 1, (i - 5) // 2)
                if not last_:
                    score(b + 1)

            nc.scalar.preload_act_table(ACT.Gelu)
            act.nop().then_inc(ev_act, RING)
            act.wait_ge(gate_in, 16)
            A(gw_flat[:, 0, :], graw, ACT.Square, accum_out=ssq[:, 0:1])
            A(ssq[:, 1:2], graw[:, 0:1], ACT.Square).then_inc(ssq_ok, 1)
            x_high(0)
            act.wait_ge(scale_ok, 1)
            A(gw_flat[:, 0, :], graw, ACT.Copy, scale=scl[:, 0:1]).then_inc(whi_ok, 1)
            squares(0, 0)
            squares(0, 1)
            for i in range(2):
                x_T(0, 0, i)
            high_part(0, 0)
            high_part(0, 1)
            score(0)
            squares(1, 0)
            squares(1, 1)
            act.wait_ge(bias_half, 1)
            act.wait_ge(spare_out, 64)
            more_weights = True
            sequence(0, 0)
            with act.Fori(0, SEQS // 2 - 2) as it:
                for v in range(2):
                    sequence(it * 2 + 1 + v, (1 + v) % 2)
            sequence(SEQS - 3, 1)
            more_weights = False
            sequence(SEQS - 2, 0)
            sequence(SEQS - 1, 1, last_=True)

            def slot(n, u):
                act.wait_ge(par_ok, n + 1)
                for j in range(KH):
                    gelu(n * KH + EV_A + j, n * KH + H_A + j, j, j, par[u][:, :])

            with act.Fori(0, SLOTS // 2) as it:
                for u in range(2):
                    slot(it * 2 + u, u)
            slot(SLOTS - 1, 0)

        @block.vector
        def _(dve):
            own = Tally(dve, dve_own)
            V = nc.vector

            def seq(ins):
                own.mark(ins)
                own.settle()

            def scales(n):
                dve.wait_ge(norm_ok, 1 if n is None else n + 2)
                seq(V.tensor_scalar(norm[:, 2:3], norm[:, 0:1], 16.0,
                                    b1max[:, 0:1] if n is None else b1red[:, bass.ds(n, 1)], ALU.mult, ALU.add))
                seq(V.tensor_scalar(pw, norm, 1e-12, None, ALU.max))
                seq(V.tensor_scalar(pw.bitcast(I32), pw.bitcast(I32), EXPONENT, None, ALU.bitwise_and))
                seq(V.reciprocal(ip, pw))
                seq(V.tensor_scalar(inv, pw, 1.0 / TOP, None, ALU.mult))
                own.mark(V.tensor_scalar(scl, ip, TOP, None, ALU.mult))
                if n is None:
                    own.mark(V.tensor_scalar(a_gate, inv[:, 0:1], 1.0 / XSCALE, None, ALU.mult))
                    V.tensor_scalar(a_half, inv[:, 0:1], 0.5 / XSCALE, None, ALU.mult).then_inc(scale_ok, 1)
                    return
                own.settle()
                own.mark(V.tensor_scalar(PT[:, bass.ds(n, 1), 0:1].squeeze(1), inv[:, 0:1], 1.0 / XSCALE, None,
                                         ALU.mult))
                own.mark(V.tensor_copy(PT[:, bass.ds(n, 1), 1:2].squeeze(1), scl[:, 2:3]))
                V.tensor_tensor(PT[:, bass.ds(n, 1), 2:3].squeeze(1), inv[:, 1:2], inv[:, 2:3],
                                ALU.mult).then_inc(scale_ok, 1)

            def low_first(n):
                o = n * WSET
                dve.wait_ge(whi_ok, n * 2 + 2)
                V.scalar_tensor_tensor(out=W[:, bass.ds(o + HALF, HALF)], in0=stage[0][:, :], scalar=scl[:, 0:1],
                                       in1=W[:, bass.ds(o, HALF)], op0=ALU.mult,
                                       op1=ALU.subtract).then_inc(stage_used[0], 1)

            def variances(b, u):
                dve.wait_ge(x_in[u], (b - u) * 8 + 16)
                for t in range(TPB):
                    own.mark(V.bn_stats(stats[:, t, :], xt[u][:, t * D:(t + 1) * D]))
                own.settle()
                V.memset(scratch, 0.0)
                for t in range(TPB):
                    own.mark(V.bn_aggr(mv[:, t, :], stats[:, t, :]))
                own.settle()
                V.tensor_scalar(ve.unsqueeze(2), mv[:, :, 1:2], EPS, XSCALE ** -2, ALU.add,
                                ALU.mult).then_inc(var_ok, 1)

            def normed(b, u):
                dve.wait_ge(rs_ok, b + 1)
                for t in range(TPB):
                    ins = V.tensor_scalar(xs[:, t * D:(t + 1) * D], xt[u][:, t * D:(t + 1) * D], mv[:, t, 0:1],
                                          rs[:, t:t + 1], ALU.subtract, ALU.mult)
                ins.then_inc(xs_ok, 1)

            def scan(b, ch):
                dve.wait_ge(ev_act, b * EVENTS + 3 * ch + 3 + RING)
                own.mark(V.scalar_tensor_tensor(out=sg[ch], in0=sg[ch], scalar=1.0, in1=tv[ch], op0=ALU.add,
                                                op1=ALU.mult))
                own.mark(V.tensor_scalar(dec, dec, 0.499, 0.5, ALU.mult, ALU.add))
                own.settle()
                V.tensor_tensor_scan(tv[ch], dec, sg[ch], 0.0, ALU.mult, ALU.add).then_inc(scan_ok, 1)

            def residual(b, u, i):
                dve.wait_ge(scanT_ps, b * 2 + i + 1 + 2)
                c = slice(i * 512, (i + 1) * 512)
                V.scalar_tensor_tensor(out=acc[:, c], in0=ps_t[:, :], scalar=0.5, in1=xt[u][:, c], op0=ALU.mult,
                                       op1=ALU.add).then_inc(r_ok, 1)

            def shared_result(b, i):
                dve.wait_ge(y_ps, (b * 2 + i + 1) * KH + RING)
                c = slice(i * 512, (i + 1) * 512)
                V.scalar_tensor_tensor(out=acc[:, c], in0=ps_y[i][:, :], scalar=PT[:, 0, 2:3], in1=acc[:, c],
                                       op0=ALU.mult, op1=ALU.add).then_inc(y_ok, 1)

            def best_two(b):
                dve.wait_ge(logit_ps, b + 1)
                seq(V.scalar_tensor_tensor(out=z, in0=ps_l[:, 0:32].rearrange("p (t e) -> p t e", e=E),
                                           scalar=a_gate, in1=gb.unsqueeze(1).to_broadcast([P, TPB, E]),
                                           op0=ALU.mult, op1=ALU.add))
                seq(V.tensor_scalar(z, z, SATURATED, None, ALU.min))
                for k, src in enumerate((z, z2)):
                    seq(V.tensor_reduce(top_z[:, k, :], src, AX.X, ALU.max))
                    seq(V.tensor_tensor(eq, src, top_z[:, k, :].unsqueeze(2).to_broadcast([P, TPB, E]), ALU.is_equal))
                    seq(V.tensor_tensor(key, eq, desc, ALU.mult))
                    seq(V.tensor_reduce(best, key, AX.X, ALU.max))
                    seq(V.tensor_tensor(oh[:, k], key, best.unsqueeze(2).to_broadcast([P, TPB, E]), ALU.is_equal))
                    if k == 0:
                        seq(V.scalar_tensor_tensor(out=z2, in0=oh[:, 0], scalar=-1e30, in1=z, op0=ALU.mult,
                                                   op1=ALU.add))
                V.tensor_tensor(mask.rearrange("p (t e) -> p t e", e=E), oh[:, 0], oh[:, 1],
                                ALU.add).then_inc(top_ok, 1)

            def places(b, u):
                dve.wait_ge(rank_ps, b + 1)
                ranks = ps_l[:, 64:96].rearrange("p (t e) -> p t e", e=E)
                seq(V.tensor_tensor(pos, ranks, carry.unsqueeze(1).to_broadcast([P, TPB, E]), ALU.add))
                own.mark(V.tensor_tensor(carry, carry, ps_l[:, 96:104], ALU.add))
                seq(V.tensor_tensor(ohp, oh, pos.unsqueeze(1).to_broadcast([P, 2, TPB, E]), ALU.mult))
                seq(V.tensor_reduce(place_f, ohp, AX.X, ALU.add))
                dve.wait_ge(entry_ok, b * 2 + 2)
                own.mark(V.tensor_copy(place[u][:, :], place_f))
                dve.wait_ge(tanh_ok, b + 1)
                v = entry[u][:, :].bitcast(F32).rearrange("p (n c) -> p n c", c=2)[:, :, 1:2]
                V.tensor_scalar(v, top_t.unsqueeze(2), 0.5, 0.5, ALU.mult, ALU.add).then_inc(place_ok, 1)

            def split_h(ev, m, i, p):
                dve.wait_ge(ev_act, ev + 1 + RING)
                dve.wait_ge(y_ps, m + 1)
                hi, lo, v = hhl[i % RING][:, 0, :], hhl[i % RING][:, 1, :], h32[i % RING]
                seq(V.tensor_scalar(hi, v, p[:, 1:2], None, ALU.mult))
                V.scalar_tensor_tensor(out=lo, in0=v, scalar=p[:, 1:2], in1=hi, op0=ALU.mult,
                                       op1=ALU.subtract).then_inc(hhl_ok, 1)

            def sequence(b, u, first=False, last_=False):
                if not first:
                    shared_result(b - 1, 1)
                if not last_:
                    variances(b + 1, 1 - u)
                    dve.wait_ge(stage_used[1], b + 1)
                    scales(b + 1)
                scan(b, 0)
                if not last_:
                    normed(b + 1, 1 - u)
                places(b, u)
                scan(b, 1)
                if last_:
                    tables()
                for i in range(2 * KH):
                    split_h(b * EVENTS + PROJ + i, b * 2 * KH + i, i, PT[:, 0, :])
                    if i == 2 and not last_:
                        low_first(b + 1)
                    if i == 4 and not first:
                        dve.wait_ge(o_out, b * 16)
                    if i in (4, 6):
                        residual(b, u, (i - 4) // 2)
                    if i == 9:
                        shared_result(b, 0)
                    if i == 11 and not last_:
                        best_two(b + 1)
                    if i == 3 and last_:
                        dve.wait_ge(stage_used[1], NW - 1)
                        scales(NW - 1)
                    if i == 8 and last_:
                        low_first(NW - 1)

            def tables():
                own.settle()
                seq(V.tensor_tensor(count, carry, ebase, ALU.subtract))
                seq(V.tensor_scalar(count_i, count, float(ROWS - 1), None, ALU.add))
                seq(V.tensor_scalar(pad_i, count_i, -ROWS, None, ALU.bitwise_and))
                seq(V.tensor_copy(pad, pad_i))
                own.mark(V.tensor_scalar(room, pad, -1.0, float(TOKENS), ALU.mult, ALU.add))
                seq(V.tensor_tensor_scan(pad_end, one, pad, 0.0, ALU.mult, ALU.add))
                seq(V.tensor_tensor(ended, pad_end.unsqueeze(1).to_broadcast([P, SLOTS, E]),
                                    starts.unsqueeze(2).to_broadcast([P, SLOTS, E]), ALU.is_le))
                own.mark(V.tensor_tensor(moved, ended, room.unsqueeze(1).to_broadcast([P, SLOTS, E]), ALU.mult))
                seq(V.tensor_reduce(sets, ended, AX.X, ALU.add))
                seq(V.tensor_scalar(slot_set[:, :], sets, float(E - 1), 1.0, ALU.min, ALU.add))
                seq(V.tensor_reduce(sets, moved, AX.X, ALU.add))
                V.tensor_tensor(slot_at[:, :], sets, starts, ALU.add).then_inc(route_ok, 1)
                dve.wait_ge(route_ok, 1)

            V.engine_nop().then_inc(y_ok, 2)
            V.engine_nop().then_inc(hhl_ok, RING)
            for e in range(E):
                own.mark(V.memset(desc[:, :, e], float(E - e)))
                own.mark(V.memset(ebase[:, e:e + 1], float(e * TOKENS)))
                own.mark(V.memset(carry[:, e:e + 1], float(e * TOKENS)))
            own.mark(V.memset(one, 1.0))
            own.mark(V.memset(scratch, 0.0))
            own.mark(V.memset(b1max, 0.0))
            own.mark(V.memset(PT[:, :, 3:4], 0.0))
            own.settle()
            variances(0, 0)
            normed(0, 0)
            scales(None)
            dve.wait_ge(whi_ok, 1)
            V.scalar_tensor_tensor(out=gw_flat[:, 1, :], in0=graw, scalar=scl[:, 0:1], in1=gw_flat[:, 0, :],
                                   op0=ALU.mult, op1=ALU.subtract).then_inc(gw_ok, 1)
            dve.wait_ge(tab_in, 64)
            V.tensor_reduce(b1max, PT[:, :, 4:NPAR], AX.X, ALU.max, apply_absolute_value=True).then_inc(b1_ok, 1)
            seq(V.tensor_tensor(gb, gb, gb2, ALU.add))
            own.mark(V.tensor_scalar(sbt[:, 0:2], sbt[:, 0:2], 0.5, None, ALU.mult))
            own.mark(V.tensor_scalar(sbt[:, 4:6], sbt[:, 4:6], 0.5, None, ALU.mult))
            dve.wait_ge(iota_ok, 1)
            seq(V.tensor_copy(starts, starts_i))
            V.engine_nop().then_inc(bias_half, 1)
            scales(0)
            low_first(0)
            best_two(0)
            sequence(0, 0, first=True)
            with own.loop(SEQS // 2 - 1, 2 * PER) as it:
                for v in range(2):
                    sequence(it * 2 + 1 + v, (1 + v) % 2)
            sequence(SEQS - 1, 1, last_=True)
            shared_result(SEQS - 1, 1)

            def parameters(n, u, first=False):
                dve.wait_ge(list_in[u], (n - u) * 8 + 16)
                if not first:
                    dve.wait_ge(add_out[u], (n - u) * 16)
                s = dve.value_load(slot_set[0:1, bass.ds(n, 1)], min_val=0, max_val=NW - 1)
                V.tensor_copy(slot_add[u][:, :, :].bitcast(I32), slot_list[u][:, :, :].bitcast(I32))
                V.tensor_copy(par[u][:, :], PT[:, bass.ds(s, 1), :].squeeze(1)).then_inc(par_ok, 1)

            def rows_T(n, u):
                dve.wait_ge(rowsT_ps, n + 1)
                V.tensor_copy(rows[1][:, u * 1024:(u + 1) * 1024].bitcast(I32),
                              ps_t[:, :].bitcast(I32)).then_inc(rowsT_ok, 1)

            def result(n, u):
                dve.wait_ge(y_ps, (n + 1) * KH + H_A + RING)
                dve.wait_ge(b2_in[u], (n - u) * 8 + 16)
                for t in range(2):
                    c = slice(t * D, (t + 1) * D)
                    own.mark(V.scalar_tensor_tensor(out=y_sb[u][:, c], in0=ps_y[u][:, c], scalar=par[u][:, 2:3],
                                                    in1=b2row[u][:, :], op0=ALU.mult, op1=ALU.add))
                own.settle()
                for t in range(2):
                    c = slice(t * D, (t + 1) * D)
                    ins = V.tensor_scalar(y_sb[u][:, c], y_sb[u][:, c], slot_add[u][:, t, 1:2].bitcast(F32), None,
                                          ALU.mult)
                ins.then_inc(y_ok, 1)

            def slot(n, u, first=False, final=False):
                for j in range(KH):
                    split_h(n * KH + EV_A + j, n * KH + H_A + j, j, par[u][:, :])
                    if j == 0 and not first:
                        result(n - 1, 1 - u)
                    if j == 3 and not final:
                        rows_T(n + 1, 1 - u)
                    if j == 4 and not final:
                        parameters(n + 1, 1 - u, first)

            parameters(0, 0, first=True)
            rows_T(0, 0)
            slot(0, 0, first=True)
            with own.loop((SLOTS - 3) // 2, 2 * (KH + 2)) as it:
                for v in range(2):
                    slot(it * 2 + 1 + v, (1 + v) % 2)
            slot(SLOTS - 2, 1)
            slot(SLOTS - 1, 0, final=True)
            result(SLOTS - 1, 0)

        @block.tensor
        def _(pe):
            T = nc.tensor
            PASSES = ((0, 0), (0, 1), (1, 0))

            def x_transposes(b, i):
                for q in range(2):
                    for t in range(TPB):
                        c = (2 * i + q) * P
                        ins = T.transpose(ps_t16[:, q * SEQ + t * P:q * SEQ + (t + 1) * P], xhl[:, t, c:c + P],
                                          ident[:, :])
                ins.then_inc(xT_ps, 1)

            def logits(b, u):
                pe.wait_ge(xT_ok, b * 2 + 2)
                for t in range(TPB):
                    for n in range(3 * KD):
                        c, (xp, wp) = n // 3, PASSES[n % 3]
                        ins = T.matmul(ps_l[:, t * E:(t + 1) * E], xT[u][:, 2 * xp + c, t * P:(t + 1) * P],
                                       gw[:, wp, c, GATES:GCOL], start=n == 0, stop=n == 3 * KD - 1)
                ins.then_inc(logit_ps, 1)

            def ranks(b):
                pe.wait_ge(top_ok, b + 1)
                for t in range(TPB + 1):
                    for v in range(min(t + 1, TPB)):
                        ins = T.matmul(ps_l[:, 64 + t * E:64 + (t + 1) * E], (before if v == t else ones)[:, :],
                                       mask[:, v * E:(v + 1) * E], start=v == 0, stop=v == min(t, TPB - 1))
                ins.then_inc(rank_ps, 1)

            def scan_transposes(b, i):
                for t in range(2 * i, 2 * i + 2):
                    for ch in range(KD):
                        o = (t % 2) * D + ch * P
                        ins = T.transpose(ps_t[:, o:o + P], tv[ch][:, t * P:(t + 1) * P], identf[:, :])
                ins.then_inc(scanT_ps, 1)

            def projection(b, u, i):
                ch, g = divmod(i, 3)
                pe.wait_ge(ev_act, b * EVENTS + i + 1)
                for n in range(3 * KD):
                    c, (xp, wp) = n // 3, PASSES[n % 3]
                    o = g * D + ch * P
                    ins = T.matmul(ps_e[(2 * u + i) % RING][:, :], gw[:, wp, c, o:o + P], xT[u][:, 2 * xp + c, :],
                                   start=n == 0, stop=n == 3 * KD - 1)
                ins.then_inc(ev_ps, 1)

            def weights(w, o, n):
                return W[:, o:o + n] if w is None else W[:, bass.ds(w + o, n)]

            def layer1(ev, k, j, rhs, w):
                pe.wait_ge(ev_act, ev + 1)
                for n in range(3 * KD):
                    c, (wp, xp) = n // 3, PASSES[n % 3]
                    ins = T.matmul(ps_e[k % RING][:, 0:ROWS], weights(w, wp * HALF + c * H + j * P, P),
                                   rhs[:, 2 * xp + c, :], start=n == 0, stop=n == 3 * KD - 1)
                ins.then_inc(ev_ps, 1)

            def layer2(m, s, i, u, w):
                pe.wait_ge(hhl_ok, m + 1 + RING)
                j = i % KH
                if j == 0:
                    pe.wait_ge(y_ok, s + 1)
                for t in range(2):
                    for hp, wp in PASSES:
                        ins = T.matmul(ps_y[u][:, t * D:(t + 1) * D], hhl[i % RING][:, hp, t * P:(t + 1) * P],
                                       weights(w, (2 + wp) * HALF + j * D, D),
                                       start=(j, t, hp, wp) == (0, 0, 0, 0), stop=(j, hp, wp) == (KH - 1, 1, 0),
                                       skip_group_check=True)
                ins.then_inc(y_ps, 1)

            def make(b, u, k):
                if k < PROJ:
                    projection(b, u, k)
                else:
                    i = k - PROJ
                    s, j = divmod(i, KH)
                    layer1(b * EVENTS + k, 2 * u + k, j, xT[u][:, :, s * ROWS:(s + 1) * ROWS], None)

            def sequence(b, u, last_=False):
                for k in range(EVENTS):
                    if k + AHEAD < EVENTS:
                        make(b, u, k + AHEAD)
                    elif not last_:
                        make(b + 1, 1 - u, k + AHEAD - EVENTS)
                    i = k - PROJ
                    if i >= 0:
                        layer2(b * 2 * KH + i, b * 2 + i // KH, i, i // KH, None)
                    if k == 1:
                        ranks(b)
                    if i == 3:
                        pe.wait_ge(scan_ok, b * 2 + 2)
                        pe.wait_ge(xT_ok, b * 2 + 2)
                        scan_transposes(b, 0)
                    if i == 5:
                        pe.wait_ge(r_ok, b * 2 + 1)
                        scan_transposes(b, 1)
                    if i == 6 and not last_:
                        pe.wait_ge(xhl_ok, b + 2)
                        pe.wait_ge(r_ok, b * 2 + 2)
                        x_transposes(b + 1, 0)
                    if i == 8 and not last_:
                        pe.wait_ge(xT_ok, b * 2 + 3)
                        x_transposes(b + 1, 1)
                    if i == 10 and not last_:
                        logits(b + 1, 1 - u)

            pe.nop().then_inc(scanT_ps, 2)
            pe.nop().then_inc(y_ps, RING)
            pe.wait_ge(const_ok, 4)
            pe.wait_ge(xhl_ok, 1)
            x_transposes(0, 0)
            pe.wait_ge(xT_ok, 1)
            x_transposes(0, 1)
            pe.wait_ge(gw_ok, 1)
            logits(0, 0)
            for k in range(AHEAD):
                make(0, 0, k)
            pe.wait_ge(stage_used[0], 1)
            pe.wait_ge(stage_used[1], 1)
            with pe.Fori(0, SEQS // 2 - 1) as it:
                for u in range(2):
                    sequence(it * 2 + u, u)
            sequence(SEQS - 2, 0)
            sequence(SEQS - 1, 1, last_=True)

            def row_transposes(n, u):
                pe.wait_ge(rows_in[u], (n - u) * 16 + 32)
                pe.wait_ge(rowsT_ok, n)
                for q in range(4):
                    for t in range(2):
                        o = q * ROWS + t * P
                        ins = T.transpose(ps_t16[:, o:o + P], xg[u][:, t, q * P:(q + 1) * P], ident[:, :])
                ins.then_inc(rowsT_ps, 1)

            def weight_set(n):
                s = pe.value_load(slot_set[0:1, bass.ds(n, 1)], min_val=0, max_val=NW - 1)
                return pe.snap(s * WSET)

            def slot(n, u, w, final=False):
                w_next = None
                for j in range(KH):
                    if j + AHEAD < KH:
                        layer1(n * KH + EV_A + j + AHEAD, j + AHEAD, j + AHEAD, xgT[u], w)
                    elif not final:
                        i = j + AHEAD - KH
                        if w_next is None:
                            pe.wait_ge(rowsT_ok, n + 2)
                            w_next = weight_set(n + 1)
                        layer1(n * KH + EV_A + j + AHEAD, i, i, xgT[1 - u], w_next)
                    layer2(n * KH + H_A + j, n + S_A, j, u, w)
                    if j == 2 and not final:
                        row_transposes(n + 1, 1 - u)

            pe.wait_ge(route_ok, 1)
            row_transposes(0, 0)
            pe.wait_ge(stage_used[0], NW)
            pe.wait_ge(stage_used[1], NW)
            pe.wait_ge(rowsT_ok, 1)
            w0 = weight_set(0)
            for j in range(AHEAD):
                layer1(EV_A + j, j, j, xgT[0], w0)
            with pe.Fori(0, SLOTS // 2) as it:
                for u in range(2):
                    slot(it * 2 + u, u, weight_set(it * 2 + u))
            slot(SLOTS - 1, 0, weight_set(SLOTS - 1), final=True)


def kernel(**inputs):
    import numpy as np
    import concourse.bacc as bacc
    from concourse.bass_utils import run_bass_kernel_spmd

    a = {k.replace("L0_", ""): np.asarray(v) for k, v in inputs.items()}
    b1 = np.concatenate([a["ffn_bs1"][None], a["ffn_b1"]])
    arrays = {
        "x": a["attn_x"].reshape(TOKENS, D),
        "w1": np.concatenate([a["ffn_Ws1"][None], a["ffn_W1"]]).transpose(0, 2, 1),
        "w2": np.concatenate([a["ffn_Ws2"][None], a["ffn_W2"]]).transpose(0, 2, 1),
        "gates": np.concatenate([a["attn_Wg"], a["attn_Wv"], a["attn_Wd"], a["ffn_Wg"].T], axis=1),
        "b1": b1.reshape(NW, KH, P).transpose(2, 0, 1),
        "b2": np.concatenate([a["ffn_bs2"][None], a["ffn_b2"]]),
        "gbias": np.stack([a["ffn_bg"], a["ffn_bias"]]),
        "sbias": np.stack([a["attn_bg"], a["attn_bv"], a["attn_bd"]]).reshape(3 * KD, P).T,
    }
    arrays = {f"in_{k}": np.ascontiguousarray(v) for k, v in arrays.items()}
    nc = bacc.Bacc("TRN2", target_bir_lowering=False, num_devices=1)
    aps = [nc.dram_tensor(k, v.shape, mybir.dt.from_np(v.dtype), kind="ExternalInput").ap() for k, v in arrays.items()]
    out = nc.dram_tensor("out", (TOKENS + ROWS, D), F32, kind="ExternalOutput").ap()
    layer(nc, *aps, out)
    r = run_bass_kernel_spmd(nc, [arrays], core_ids=[0])
    return r.results[0]["out"][:TOKENS].reshape(SEQS, SEQ, D)
```

```python
from contextlib import ExitStack, contextmanager

import concourse.bass as bass
from concourse import mybir

F32, F16, I32, U32 = mybir.dt.float32, mybir.dt.float16, mybir.dt.int32, mybir.dt.uint32
ALU, ACT, AX = mybir.AluOpType, mybir.ActivationFunctionType, mybir.AxisListType
RMAX, RADD = bass.bass_isa.ReduceOp.max, bass.bass_isa.ReduceOp.add

P = 128
SEQS, SEQ, D, H, E = 8, 512, 256, 1024, 8
TOKENS = SEQS * SEQ
TPB = SEQ // P
KD, KH = D // P, H // P
ROWS = 256
SLOTS = 2 * TOKENS // ROWS + E - 1
LIST = E * TOKENS + (E - 1) * ROWS
NW = E + 1
HALF = KD * H
WSET = 4 * HALF
GATES = 3 * D
GCOL = GATES + E
XSCALE = 256.0
TOP = 2.0 ** 14
EXPONENT = 0x7F800000
EPS = 1e-5
SATURATED = 17.5
RING = 4
AHEAD = 3
PROJ = 6
EVENTS = PROJ + 2 * KH
EV_A, H_A, S_A = SEQS * EVENTS, SEQS * 2 * KH, 2 * SEQS
PER = 54
NPAR = 12


class Tally:

    def __init__(self, eng, sem):
        self.eng, self.sem, self.base, self.k = eng, sem, 0, 0

    def mark(self, ins):
        ins.then_inc(self.sem, 1)
        self.k += 1

    def settle(self):
        self.eng.wait_ge(self.sem, self.base + self.k)

    @contextmanager
    def loop(self, trips, per):
        start = self.k
        assert not self.base
        with self.eng.Fori(0, trips) as i:
            self.base, self.k = i * per + start, 0
            yield i
            assert self.k == per, self.k
        self.base, self.k = 0, start + trips * per


def layer(nc, x, w1, w2, gates, b1, b2, gbias, sbias, out):
    ctx = ExitStack()
    with ctx:
        def sb(name, shape, dt):
            return ctx.enter_context(nc.sbuf_tensor(name, shape, dt))

        def sem(name):
            return ctx.enter_context(nc.semaphore(name))

        xhl_dram = nc.dram_tensor("xhl_rows", (TOKENS + ROWS, 2 * D), F16, kind="Internal").ap()
        list_dram = nc.dram_tensor("lists", (LIST, 2), U32, kind="Internal").ap()

        W = sb("W", [P, NW * WSET], F16)
        PT = sb("PT", [P, NW, NPAR], F32)
        par = [sb(f"par{i}", [P, NPAR], F32) for i in range(2)]
        b2row = [sb(f"b2row{i}", [P, D], F32) for i in range(2)]
        stage = [sb(f"stage{i}", [P, HALF], F32) for i in range(2)]
        rows = [sb(f"rows{i}", [P, 4 * SEQ], F16) for i in range(2)]
        arena = sb("arena", [P, 7680], F32)
        small = sb("small", [P, 256], F32)
        rt = sb("rt", [P, 480], F32)
        bs2 = sb("bs2", [P, D], F32)
        ident = sb("ident", [P, P], F16)
        identf = sb("identf", [P, P], F32)
        before = sb("before", [P, P], F16)
        ones = sb("ones", [P, P], F16)
        token = sb("token", [P, SEQS * TPB], U32)
        entry = [sb(f"entry{i}", [P, 4 * TPB], U32) for i in range(2)]
        place = [sb(f"place{i}", [P, 2 * TPB], U32) for i in range(2)]
        slot_list = [sb(f"slot_list{i}", [P, 2, 2], U32) for i in range(2)]
        slot_add = [sb(f"slot_add{i}", [P, 2, 2], U32) for i in range(2)]
        slot_set = sb("slot_set", [P, SLOTS], I32)
        slot_at = sb("slot_at", [P, SLOTS], I32)

        xT = [r[:, :].rearrange("p (q n) -> p q n", q=4) for r in rows]
        xg = [rows[0][:, i * 1024:(i + 1) * 1024].rearrange("p (t n) -> p t n", t=2) for i in range(2)]
        xgT = [rows[1][:, i * 1024:(i + 1) * 1024].rearrange("p (q n) -> p q n", q=4) for i in range(2)]
        h32 = [arena[:, i * ROWS:(i + 1) * ROWS] for i in range(RING)]
        hhl = [arena[:, 1024 + i * ROWS:1024 + (i + 1) * ROWS].bitcast(F16).rearrange(
            "p (s n) -> p s n", s=2) for i in range(RING)]
        xt = [arena[:, 2048 + i * 1024:3072 + i * 1024] for i in range(2)]
        acc = arena[:, 4096:5120]
        sg = [arena[:, 5120 + i * 512:5632 + i * 512] for i in range(2)]
        tv = [arena[:, 6144 + i * 512:6656 + i * 512] for i in range(2)]
        dec = arena[:, 7168:7680]
        graw = arena[:, 4096:4096 + KD * GCOL]
        spare = arena[:, 6144:6656].bitcast(U32)
        zeros = arena[:, 6656:7168]
        y_sb = [arena[:, 2048 + i * 512:2560 + i * 512] for i in range(2)]
        last = (NW - 1) * WSET
        gw_flat = W[:, last:last + 2 * KD * GCOL].rearrange("p (s n) -> p s n", s=2)
        gw = W[:, last:last + 2 * KD * GCOL].rearrange("p (s c n) -> p s c n", s=2, c=KD)
        at = last + 2 * KD * GCOL
        xhl = W[:, at:at + 4 * SEQ].rearrange("p (t n) -> p t n", t=TPB)
        xs = W[:, at + 4 * SEQ:at + 8 * SEQ].bitcast(F32)
        assert at + 8 * SEQ <= NW * WSET

        early = W[:, (NW - 2) * WSET:(NW - 1) * WSET].bitcast(F32)

        def landing(n, l):
            return early[:, l * HALF:(l + 1) * HALF] if isinstance(n, int) and n == 1 else stage[l][:, :]

        stats = small[:, 0:24].rearrange("p (t n) -> p t n", t=TPB)
        mv = small[:, 24:32].rearrange("p (t n) -> p t n", t=TPB)
        ve, rs, neghalf, half = small[:, 32:36], small[:, 36:40], small[:, 40:44], small[:, 44:46]
        ssq, ssum, total, norm = small[:, 234:238], small[:, 238:242], small[:, 48:50], small[:, 50:53]
        pw, ip, scl, inv = small[:, 56:59], small[:, 60:63], small[:, 64:67], small[:, 68:71]
        a_gate, a_half = small[:, 72:73], small[:, 73:74]
        b1max, b1red = small[:, 80:89], small[:, 90:99]
        gb, gb2 = small[:, 100:108], small[:, 108:116]
        sbt = small[:, 116:122]
        count = small[:, 124:132]
        count_i, pad_i = small[:, 132:140].bitcast(I32), small[:, 140:148].bitcast(I32)
        pad, pad_end, room = small[:, 148:156], small[:, 156:164], small[:, 164:172]
        scratch = small[:, 172:173]
        carry, ebase = small[:, 176:184], small[:, 184:192]
        one = small[:, 192:200]
        top_z = small[:, 200:208].rearrange("p (k t) -> p k t", k=2)
        top_t = small[:, 208:216]
        best = small[:, 216:220]
        place_f = small[:, 220:228]
        scratch_a, scratch_p = small[:, 228:229], small[:, 230:232]

        def table(a, b):
            return rt[:, a:b].rearrange("p (t e) -> p t e", e=E)

        z, eq, key, z2, pos, desc = (table(i * 32, i * 32 + 32) for i in range(6))
        oh = rt[:, 192:256].rearrange("p (k t e) -> p k t e", k=2, e=E)
        ohp = rt[:, 256:320].rearrange("p (k t e) -> p k t e", k=2, e=E)
        mask = rt[:, 320:336].bitcast(F16)
        starts, starts_i = rt[:, 340:340 + SLOTS], rt[:, 380:380 + SLOTS].bitcast(I32)
        sets = rt[:, 420:420 + SLOTS]
        ended = arena[:, 2048:2048 + SLOTS * E].rearrange("p (i e) -> p i e", e=E)
        moved = arena[:, 2560:2560 + SLOTS * E].rearrange("p (i e) -> p i e", e=E)

        bank = [ctx.enter_context(nc.psum_tensor(f"bank{i}", [P, 512], F32)) for i in range(8)]
        ps_e = bank[0:4]
        ps_y = bank[4:6]
        ps_t = bank[6]
        ps_t16 = ps_t[:, :].bitcast(F16)
        ps_l = bank[7]

        x_in = [sem(f"x_in{i}") for i in range(2)]
        w_in = [sem(f"w_in{i}") for i in range(2)]
        early_in = [sem(f"early_in{i}") for i in range(2)]
        gate_in, tab_in, bs2_in = sem("gate_in"), sem("tab_in"), sem("bs2_in")
        const_ok = sem("const_ok")
        spare_ok = sem("spare_ok")
        spare_out = sem("spare_out")
        stage_used = [sem(f"stage_used{i}") for i in range(2)]
        gw_ok = sem("gw_ok")
        ssq_ok, norm_ok, scale_ok, whi_ok = sem("ssq_ok"), sem("norm_ok"), sem("scale_ok"), sem("whi_ok")
        var_ok, rs_ok, xs_ok, xhi_ok, xhl_ok = (sem(n) for n in ("var_ok", "rs_ok", "xs_ok", "xhi_ok", "xhl_ok"))
        bias_ok = sem("bias_ok")
        b1_ok, iota_ok, bias_half = sem("b1_ok"), sem("iota_ok"), sem("bias_half")
        xhl_out = sem("xhl_out")
        xT_ps, xT_ok = sem("xT_ps"), sem("xT_ok")
        logit_ps, top_ok, tanh_ok, mask_ok, rank_ps = (
            sem(n) for n in ("logit_ps", "top_ok", "tanh_ok", "mask_ok", "rank_ps"))
        place_ok, entry_ok = sem("place_ok"), sem("entry_ok")
        list_out = [sem(f"list_out{i}") for i in range(2)]
        ev_ps, ev_act = sem("ev_ps"), sem("ev_act")
        hhl_ok, y_ps, y_ok = sem("hhl_ok"), sem("y_ps"), sem("y_ok")
        scan_ok, scanT_ps, r_ok = sem("scan_ok"), sem("scanT_ps"), sem("r_ok")
        o_out = sem("o_out")
        route_ok = sem("route_ok")
        list_in = [sem(f"list_in{i}") for i in range(2)]
        b2_in = [sem(f"b2_in{i}") for i in range(2)]
        rows_in = [sem(f"rows_in{i}") for i in range(2)]
        add_ok, entries_ok = sem("add_ok"), sem("entries_ok")
        rowsT_ps, rowsT_ok, par_ok = sem("rowsT_ps"), sem("rowsT_ok"), sem("par_ok")
        add_out = [sem(f"add_out{i}") for i in range(2)]
        dve_own, pool_own = sem("dve_own"), sem("pool_own")

        block = ctx.enter_context(nc.Block())

        x_v = x.rearrange("(b t p) d -> b p t d", t=TPB, p=P)
        xhl_v = xhl_dram[0:TOKENS].rearrange("(b t p) d -> b p t d", t=TPB, p=P)
        out_v = out[0:TOKENS].rearrange("(b t p) d -> b p t d", t=TPB, p=P)
        w1_v = w1.rearrange("e (c p) h -> e p c h", p=P)
        w2_v = w2.rearrange("e (j p) d -> e p j d", p=P)

        def chunks(ap, n):
            return ap.rearrange("p (t n) -> p t n", t=n)

        @block.sync
        def _(sp):
            def load_x(b):
                sp.dma_start(chunks(xt[b % 2], TPB), x_v[b]).then_inc(x_in[b % 2], 16)

            def load_w(layer_, n):
                sp.dma_start(chunks(landing(n, layer_), (KD, KH)[layer_]),
                             (w1_v, w2_v)[layer_][n]).then_inc((early_in if n == 1 else w_in)[layer_], 16)

            load_x(0)
            sp.dma_start(chunks(graw, KD), gates.rearrange("(c p) n -> p c n", p=P)).then_inc(gate_in, 16)
            load_w(0, 0)
            load_w(1, 0)
            sp.dma_start(PT[:, :, 4:NPAR], b1).then_inc(tab_in, 16)
            sp.dma_start(gb, gbias[0].partition_broadcast(P)).then_inc(tab_in, 16)
            sp.dma_start(gb2, gbias[1].partition_broadcast(P)).then_inc(tab_in, 16)
            sp.dma_start(sbt, sbias).then_inc(tab_in, 16)
            sp.dma_start(bs2[:, :], b2[0].partition_broadcast(P)).then_inc(bs2_in, 16)
            load_x(1)
            for l in range(2):
                load_w(l, 1)
            sp.wait_ge(spare_ok, 2)
            list_v = list_dram.rearrange("(b r) c -> b (r c)", r=ROWS)
            sp.dma_start(list_v[0:P], spare).then_inc(spare_out, 16)
            sp.dma_start(list_v[P:LIST // ROWS], spare[0:LIST // ROWS - P]).then_inc(spare_out, 16)
            sp.dma_start(xhl_dram[TOKENS:].rearrange("(p t) d -> p (t d)", t=2),
                         zeros.bitcast(F16)).then_inc(spare_out, 16)
            sp.dma_start(out[TOKENS:].rearrange("(p t) d -> p (t d)", t=2), zeros).then_inc(spare_out, 16)

            def store_xhl(b):
                sp.wait_ge(xhl_ok, b + 1)
                sp.dma_start(xhl_v[b], xhl).then_inc(xhl_out, 16)

            def store_base(b):
                sp.wait_ge(y_ok, 2 * b + 2 + 2)
                sp.dma_start(out_v[b], chunks(acc, TPB)).then_inc(o_out, 16)

            def next_weights(n):
                for l in range(2):
                    sp.wait_ge(stage_used[l], n if n > 2 else 1)
                    load_w(l, n)

            store_xhl(0)
            for b in range(SEQS):
                if b:
                    store_base(b - 1)
                if b + 2 < NW:
                    next_weights(b + 2)
                if b + 2 < SEQS:
                    sp.wait_ge(r_ok, 2 * b + 2)
                    load_x(b + 2)
                if b + 1 < SEQS:
                    store_xhl(b + 1)
                if b == SEQS - 1:
                    sp.wait_ge(route_ok, 1)
                    for u in range(2):
                        sp.wait_ge(list_out[u], SEQS // 2 * 2 * TPB * 16)
                    sp.wait_ge(spare_out, 64)

                    def look_up(n):
                        return (sp.value_load(slot_at[0:1, bass.ds(n, 1)], min_val=0, max_val=LIST - ROWS),
                                sp.value_load(slot_set[0:1, bass.ds(n, 1)], min_val=0, max_val=NW - 1))

                    def entries(a, u):
                        sp.dma_start(slot_list[u][:, :, :], list_dram[bass.ds(a, ROWS), :].rearrange(
                            "(p t) c -> p t c", t=2)).then_inc(list_in[u], 16)

                    def second_bias(s, u):
                        sp.dma_start(b2row[u][:, :].unsqueeze(1),
                                     b2[bass.ds(s, 1), :].partition_broadcast(P)).then_inc(b2_in[u], 16)

                    for u in range(2):
                        a, s = look_up(u)
                        entries(a, u)
                        second_bias(s, u)
                    store_base(b)

            def slot(n, u):
                a, s = look_up(n)
                sp.wait_ge(rowsT_ps, n - 1)
                sp.wait_ge(entries_ok, n - 1)
                entries(a, u)
                sp.wait_ge(y_ok, S_A + n - 1 + 2)
                second_bias(s, u)

            with sp.Fori(0, (SLOTS - 3) // 2) as it:
                for u in range(2):
                    slot(it * 2 + 2 + u, u)
            slot(SLOTS - 1, 0)
            sp.wait_ge(o_out, 16 * SEQS)

        @block.gpsimd
        def _(pool):
            own = Tally(pool, pool_own)

            def made(ins):
                own.mark(ins)

            made(pool.memset(neghalf, -0.5))
            made(pool.memset(half, 0.5))
            made(pool.memset(ident[:, :], 0.0))
            made(pool.memset(identf[:, :], 0.0))
            made(pool.memset(before[:, :], 0.0))
            pool.memset(ones[:, :], 1.0).then_inc(const_ok, 1)
            own.settle()
            for m in (ident, identf):
                pool.affine_select(out=m[:, :], in_=m[:, :], compare_op=ALU.not_equal, fill=1.0, base=0,
                                   pattern=[[-1, P]], channel_multiplier=1).then_inc(const_ok, 1)
            pool.affine_select(out=before[:, :], in_=before[:, :], compare_op=ALU.is_ge, fill=1.0, base=0,
                               pattern=[[-1, P]], channel_multiplier=1).then_inc(const_ok, 1)

            def rstd(b):
                pool.wait_ge(var_ok, b + 1)
                pool.tensor_tensor(out=rs, in0=ve, in1=neghalf, op=ALU.pow).then_inc(rs_ok, 1)

            def norms(n):
                pool.wait_ge(ssq_ok, n + 1)
                made(pool.partition_all_reduce(ssum, ssq, P, RADD))
                own.settle()
                made(pool.tensor_tensor(out=total, in0=ssum[:, 0:4:2], in1=ssum[:, 1:4:2], op=ALU.add))
                own.settle()
                pool.tensor_tensor(out=norm[:, 0:2], in0=total, in1=half, op=ALU.pow).then_inc(norm_ok, 1)

            def low_second(n):
                o = n * WSET + 2 * HALF
                pool.wait_ge(whi_ok, 2 * n + 3)
                v = landing(n, 1)
                made(pool.tensor_scalar(v, v, scl[:, 1:2], None, ALU.mult))
                own.settle()
                pool.tensor_tensor(out=W[:, o + HALF:o + 2 * HALF], in0=v, in1=W[:, o:o + HALF],
                                   op=ALU.subtract).then_inc(stage_used[1], 1)

            def x_low(b):
                pool.wait_ge(xhi_ok, b + 1)
                pool.tensor_tensor(out=xhl[:, :, D:2 * D], in0=chunks(xs, TPB), in1=xhl[:, :, 0:D],
                                   op=ALU.subtract).then_inc(xhl_ok, 1)

            def add_bias(b):
                v = chunks(xt[b % 2], TPB)
                pool.tensor_tensor(out=v, in0=v, in1=bs2[:, :].unsqueeze(1).to_broadcast([P, TPB, D]),
                                   op=ALU.add).then_inc(bias_ok, 1)

            def fill_entries(b):
                u = b % 2
                if b >= 2:
                    pool.wait_ge(list_out[u], b // 2 * 2 * TPB * 16)
                for k in range(2):
                    v = entry[u][:, :].rearrange("p (k t c) -> p k t c", k=2, c=2)[:, k, :, 0]
                    pool.tensor_copy(v, token[:, b * TPB:(b + 1) * TPB]).then_inc(entry_ok, 1)

            def scatter(b):
                u = b % 2
                pool.wait_ge(entry_ok, 2 * b + 2)
                pool.wait_ge(place_ok, b + 1)
                for c in range(2 * TPB):
                    pool.indirect_dma_start(
                        list_dram, bass.IndirectOffsetOnAxis(ap=place[u][:, c:c + 1], axis=0),
                        entry[u][:, 2 * c:2 * c + 2], None).then_inc(list_out[u], 16)

            rstd(0)
            norms(0)
            made(pool.iota(spare.rearrange("p (r c) -> p r c", c=2)[:, :, 0], pattern=[[1, ROWS]], base=TOKENS,
                           channel_multiplier=0))
            pool.memset(spare.rearrange("p (r c) -> p r c", c=2)[:, :, 1], 0).then_inc(spare_ok, 1)
            pool.memset(zeros, 0.0).then_inc(spare_ok, 1)
            made(pool.iota(token[:, :], pattern=[[P, SEQS * TPB]], base=0, channel_multiplier=1))
            made(pool.iota(starts_i, pattern=[[ROWS, SLOTS]], base=0, channel_multiplier=0))
            own.settle()
            pool.nop().then_inc(iota_ok, 1)
            fill_entries(0)
            x_low(0)
            pool.wait_ge(b1_ok, 1)
            made(pool.partition_all_reduce(b1red, b1max, P, RMAX))
            own.settle()
            norms(1)
            pool.wait_ge(bs2_in, 16)
            add_bias(0)
            pool.wait_ge(spare_out, 64)
            for b in range(SEQS):
                if b + 2 < NW:
                    norms(b + 2)
                if b + 1 < SEQS:
                    rstd(b + 1)
                    x_low(b + 1)
                    add_bias(b + 1)
                    low_second(b + 1)
                scatter(b)
                if b + 1 < SEQS:
                    fill_entries(b + 1)
                if b + 1 == SEQS:
                    norms(NW)

            def hold():
                own.settle()
                made(pool.tensor_tensor(out=scratch_p, in0=half, in1=half, op=ALU.mult))

            def gather(n, u, wait=True):
                if wait:
                    pool.wait_ge(rowsT_ps, n - 1)
                pool.wait_ge(list_in[u], (n - u) * 8 + 16)
                if wait:
                    hold()
                for t in range(2):
                    pool.indirect_dma_start(
                        xg[u][:, t, :], None, xhl_dram,
                        bass.IndirectOffsetOnAxis(ap=slot_list[u][:, t, 0:1], axis=0)).then_inc(rows_in[u], 16)

            def scatter_add(n, u, wait=True):
                pool.wait_ge(add_ok, n + 1)
                if wait:
                    pool.wait_ge(add_out[1 - u], (n + u) * 16)
                hold()
                for t in range(2):
                    pool.indirect_dma_start(
                        out, bass.IndirectOffsetOnAxis(ap=slot_add[u][:, t, 0:1], axis=0),
                        y_sb[u][:, t * D:(t + 1) * D], None, compute_op=ALU.add).then_inc(add_out[u], 16)

            pool.wait_ge(xhl_out, 16 * SEQS)
            pool.wait_ge(ev_ps, EVENTS * (SEQS - 1))
            gather(0, 0, wait=False)
            gather(1, 1, wait=False)
            for u in range(2):
                gather(2 + u, u)
                if u == 0:
                    pool.wait_ge(o_out, 16 * SEQS)
                scatter_add(u, u, wait=u > 0)
            with own.loop((SLOTS - 5) // 2, 4) as it:
                for u in range(2):
                    gather(it * 2 + 4 + u, u)
                    scatter_add(it * 2 + 2 + u, u)
            gather(SLOTS - 1, 0)
            for n in range(SLOTS - 3, SLOTS):
                scatter_add(n, n % 2)
            for u in range(2):
                pool.wait_ge(add_out[u], 32 * ((SLOTS + 1 - u) // 2))

        @block.scalar
        def _(act):
            A = nc.scalar.activation

            def squares(n, l, part):
                if part == 0:
                    if isinstance(n, int) and n < 2:
                        act.wait_ge((w_in, early_in)[n][l], 16)
                    else:
                        act.wait_ge(w_in[l], n * 16)
                    if l == 0:
                        act.wait_ge(norm_ok, n + 1)
                o = n * WSET + l * 2 * HALF + part * HALF // 2
                ins = A(W[:, bass.ds(o, HALF // 2)], landing(n, l)[:, part * HALF // 2:(part + 1) * HALF // 2],
                        ACT.Square, accum_out=ssq[:, 2 * l + part:2 * l + part + 1])
                if (l, part) == (1, 1):
                    ins.then_inc(ssq_ok, 1)

            def high_part(n, l, part):
                if (l, part) == (0, 0):
                    act.wait_ge(scale_ok, n + 2)
                    A(scratch_a, half[:, 0:1], ACT.Copy)
                o = n * WSET + l * 2 * HALF + part * HALF // 2
                ins = A(W[:, bass.ds(o, HALF // 2)], landing(n, l)[:, part * HALF // 2:(part + 1) * HALF // 2],
                        ACT.Copy, scale=scl[:, l:l + 1])
                if part:
                    ins.then_inc(whi_ok, 1)

            def x_high(b):
                act.wait_ge(xs_ok, b + 1)
                A(xhl[:, :, 0:D], chunks(xs, TPB), ACT.Copy).then_inc(xhi_ok, 1)

            def x_T(b, u, i):
                act.wait_ge(xT_ps, b * 2 + i + 1)
                A(xT[u][:, 2 * i:2 * i + 2, :], chunks(ps_t16, 2), ACT.Copy).then_inc(xT_ok, 1)

            def score(b):
                act.wait_ge(top_ok, b + 1)
                A(top_t, small[:, 200:208], ACT.Tanh, scale=0.5).then_inc(tanh_ok, 1)

            def projection(b, u, i):
                ch, g = divmod(i, 3)
                act.wait_ge(ev_ps, b * EVENTS + i + 1)
                if g == 0:
                    act.wait_ge(scanT_ps, b * 2 + 2)
                if i == 5:
                    act.wait_ge(scan_ok, b * 2 + 1)
                A((sg[ch], tv[ch], dec)[g], ps_e[(2 * u + i) % RING][:, :], ACT.Tanh,
                  bias=sbt[:, 2 * g + ch:2 * g + ch + 1], scale=(a_half, a_gate, a_half)[g]).then_inc(ev_act, 1)

            def gelu(ev, m, i, k, p):
                act.wait_ge(ev_ps, ev + 1)
                act.wait_ge(hhl_ok, m + 1)
                A(h32[i % RING], ps_e[k % RING][:, 0:ROWS], ACT.Gelu, bias=p[:, 4 + i % KH:5 + i % KH],
                  scale=p[:, 0:1]).then_inc(ev_act, 1)

            def rows_T(n, u):
                act.wait_ge(rowsT_ps, n + 1)
                A(rows[1][:, u * 1024:(u + 1) * 1024], ps_t16, ACT.Copy).then_inc(rowsT_ok, 1)

            def sequence(b, u, last_=False):
                for i in range(PROJ):
                    projection(b, u, i)
                    if not last_:
                        if i in (2, 3):
                            high_part(b + 1, 0, i - 2)
                if last_:
                    act.wait_ge(xhl_out, 16 * SEQS)
                for i in range(2 * KH):
                    gelu(b * EVENTS + PROJ + i, b * 2 * KH + i, i, 2 * u + PROJ + i, PT[:, 0, :])
                    if not last_:
                        if i == 0:
                            act.wait_ge(xhl_out, b * 16 + 16)
                            x_high(b + 1)
                        if i in (2, 4):
                            high_part(b + 1, 1, i // 2 - 1)
                        if i in (8, 10):
                            x_T(b + 1, 1 - u, (i - 8) // 2)
                        if 11 <= i < 15 and more_weights:
                            squares(b + 2, (i - 11) // 2, (i - 11) % 2)
                    elif i < 4:
                        squares(NW - 1, i // 2, i % 2)
                    elif 5 <= i < 9:
                        high_part(NW - 1, (i - 5) // 2, (i - 5) % 2)
                    if i == 13 and last_:
                        rows_T(0, 0)
                if not last_:
                    score(b + 1)

            nc.scalar.preload_act_table(ACT.Gelu)
            act.nop().then_inc(ev_act, RING)
            act.wait_ge(gate_in, 16)
            for part in range(2):
                c = slice(part * GCOL, (part + 1) * GCOL)
                A(gw_flat[:, 0, c], graw[:, c], ACT.Square, accum_out=ssq[:, part:part + 1])
            A(ssq[:, 2:4], graw[:, 0:2], ACT.Square).then_inc(ssq_ok, 1)
            x_high(0)
            act.wait_ge(scale_ok, 1)
            A(gw_flat[:, 0, :], graw, ACT.Copy, scale=scl[:, 0:1]).then_inc(whi_ok, 1)
            for part in range(4):
                squares(0, part // 2, part % 2)
            for i in range(2):
                x_T(0, 0, i)
            for part in range(4):
                high_part(0, part // 2, part % 2)
            for part in range(4):
                squares(1, part // 2, part % 2)
            score(0)
            act.wait_ge(bias_half, 1)
            act.wait_ge(spare_out, 64)
            more_weights = True
            sequence(0, 0)
            with act.Fori(0, SEQS // 2 - 2) as it:
                for v in range(2):
                    sequence(it * 2 + 1 + v, (1 + v) % 2)
            sequence(SEQS - 3, 1)
            more_weights = False
            sequence(SEQS - 2, 0)
            sequence(SEQS - 1, 1, last_=True)

            def weigh(n, u):
                act.wait_ge(y_ok, S_A + n + 1 + 2)
                for t in range(2):
                    y = y_sb[u][:, t * D:(t + 1) * D]
                    ins = A(y, y, ACT.Copy, scale=slot_add[u][:, t, 1:2].bitcast(F32))
                ins.then_inc(add_ok, 1)

            def slot(n, u, first=False, final=False):
                act.wait_ge(par_ok, n + 1)
                for j in range(KH):
                    gelu(n * KH + EV_A + j, n * KH + H_A + j, j, j, par[u][:, :])
                    if j == 2 and not first:
                        weigh(n - 1, 1 - u)
                    if j == 4 and not final:
                        rows_T(n + 1, 1 - u)

            slot(0, 0, first=True)
            with act.Fori(0, (SLOTS - 3) // 2) as it:
                for v in range(2):
                    slot(it * 2 + 1 + v, (1 + v) % 2)
            slot(SLOTS - 2, 1)
            slot(SLOTS - 1, 0, final=True)
            weigh(SLOTS - 1, 0)

        @block.vector
        def _(dve):
            own = Tally(dve, dve_own)
            V = nc.vector

            def seq(ins):
                own.mark(ins)
                own.settle()

            def scales(n):
                dve.wait_ge(norm_ok, 1 if n is None else n + 2)
                seq(V.tensor_scalar(norm[:, 2:3], norm[:, 0:1], 16.0,
                                    b1max[:, 0:1] if n is None else b1red[:, bass.ds(n, 1)], ALU.mult, ALU.add))
                seq(V.tensor_scalar(pw, norm, 1e-12, None, ALU.max))
                seq(V.tensor_scalar(pw.bitcast(I32), pw.bitcast(I32), EXPONENT, None, ALU.bitwise_and))
                seq(V.reciprocal(ip, pw))
                seq(V.tensor_scalar(inv, pw, 1.0 / TOP, None, ALU.mult))
                own.mark(V.tensor_scalar(scl, ip, TOP, None, ALU.mult))
                if n is None:
                    own.mark(V.tensor_scalar(a_gate, inv[:, 0:1], 1.0 / XSCALE, None, ALU.mult))
                    V.tensor_scalar(a_half, inv[:, 0:1], 0.5 / XSCALE, None, ALU.mult).then_inc(scale_ok, 1)
                    return
                own.settle()
                own.mark(V.tensor_scalar(PT[:, bass.ds(n, 1), 0:1].squeeze(1), inv[:, 0:1], 1.0 / XSCALE, None,
                                         ALU.mult))
                own.mark(V.tensor_copy(PT[:, bass.ds(n, 1), 1:2].squeeze(1), scl[:, 2:3]))
                V.tensor_tensor(PT[:, bass.ds(n, 1), 2:3].squeeze(1), inv[:, 1:2], inv[:, 2:3],
                                ALU.mult).then_inc(scale_ok, 1)

            def low_part(n, l, part):
                if part == 0:
                    dve.wait_ge(whi_ok, n * 2 + 2 + l)
                o = n * WSET + l * 2 * HALF + part * HALF // 2
                ins = V.scalar_tensor_tensor(out=W[:, bass.ds(o + HALF, HALF // 2)],
                                             in0=landing(n, l)[:, part * HALF // 2:(part + 1) * HALF // 2],
                                             scalar=scl[:, l:l + 1], in1=W[:, bass.ds(o, HALF // 2)], op0=ALU.mult,
                                             op1=ALU.subtract)
                if part:
                    ins.then_inc(stage_used[l], 1)

            def variances(b, u):
                dve.wait_ge(x_in[u], (b - u) * 8 + 16)
                for t in range(TPB):
                    own.mark(V.bn_stats(stats[:, t, :], xt[u][:, t * D:(t + 1) * D]))
                own.settle()
                V.memset(scratch, 0.0)
                for t in range(TPB):
                    own.mark(V.bn_aggr(mv[:, t, :], stats[:, t, :]))
                own.settle()
                V.tensor_scalar(ve.unsqueeze(2), mv[:, :, 1:2], EPS, XSCALE ** -2, ALU.add,
                                ALU.mult).then_inc(var_ok, 1)

            def normed(b, u):
                dve.wait_ge(rs_ok, b + 1)
                for t in range(TPB):
                    ins = V.tensor_scalar(xs[:, t * D:(t + 1) * D], xt[u][:, t * D:(t + 1) * D], mv[:, t, 0:1],
                                          rs[:, t:t + 1], ALU.subtract, ALU.mult)
                ins.then_inc(xs_ok, 1)

            def scan_input(b, ch):
                dve.wait_ge(ev_act, b * EVENTS + 3 * ch + 3 + RING)
                own.mark(V.scalar_tensor_tensor(out=sg[ch], in0=sg[ch], scalar=1.0, in1=tv[ch], op0=ALU.add,
                                                op1=ALU.mult))
                own.mark(V.tensor_scalar(dec, dec, 0.499, 0.5, ALU.mult, ALU.add))

            def scan(ch):
                own.settle()
                V.tensor_tensor_scan(tv[ch], dec, sg[ch], 0.0, ALU.mult, ALU.add).then_inc(scan_ok, 1)

            def residual(b, u, i):
                dve.wait_ge(scanT_ps, b * 2 + i + 1 + 2)
                c = slice(i * 512, (i + 1) * 512)
                V.scalar_tensor_tensor(out=acc[:, c], in0=ps_t[:, :], scalar=0.5, in1=xt[u][:, c], op0=ALU.mult,
                                       op1=ALU.add).then_inc(r_ok, 1)

            def shared_result(b, i):
                dve.wait_ge(y_ps, (b * 2 + i + 1) * KH + RING)
                c = slice(i * 512, (i + 1) * 512)
                V.scalar_tensor_tensor(out=acc[:, c], in0=ps_y[i][:, :], scalar=PT[:, 0, 2:3], in1=acc[:, c],
                                       op0=ALU.mult, op1=ALU.add).then_inc(y_ok, 1)

            def best_two(b, part):
                if part == 0:
                    dve.wait_ge(logit_ps, b + 1)
                    seq(V.scalar_tensor_tensor(out=z, in0=ps_l[:, 0:32].rearrange("p (t e) -> p t e", e=E),
                                               scalar=a_gate, in1=gb.unsqueeze(1).to_broadcast([P, TPB, E]),
                                               op0=ALU.mult, op1=ALU.add))
                    seq(V.tensor_scalar(z, z, SATURATED, None, ALU.min))
                elif part in (1, 3):
                    k, src = part // 2, (z, z2)[part // 2]
                    seq(V.tensor_reduce(top_z[:, k, :], src, AX.X, ALU.max))
                    seq(V.tensor_tensor(eq, src, top_z[:, k, :].unsqueeze(2).to_broadcast([P, TPB, E]),
                                        ALU.is_equal))
                    seq(V.tensor_tensor(key, eq, desc, ALU.mult))
                else:
                    k = part // 2 - 1
                    seq(V.tensor_reduce(best, key, AX.X, ALU.max))
                    seq(V.tensor_tensor(oh[:, k], key, best.unsqueeze(2).to_broadcast([P, TPB, E]), ALU.is_equal))
                    if k == 0:
                        seq(V.scalar_tensor_tensor(out=z2, in0=oh[:, 0], scalar=-1e30, in1=z, op0=ALU.mult,
                                                   op1=ALU.add))
                    else:
                        V.tensor_tensor(mask.rearrange("p (t e) -> p t e", e=E), oh[:, 0], oh[:, 1],
                                        ALU.add).then_inc(top_ok, 1)

            def places(b, u):
                dve.wait_ge(rank_ps, b + 1)
                ranks = ps_l[:, 64:96].rearrange("p (t e) -> p t e", e=E)
                seq(V.tensor_tensor(pos, ranks, carry.unsqueeze(1).to_broadcast([P, TPB, E]), ALU.add))
                own.mark(V.tensor_tensor(carry, carry, ps_l[:, 96:104], ALU.add))
                seq(V.tensor_tensor(ohp, oh, pos.unsqueeze(1).to_broadcast([P, 2, TPB, E]), ALU.mult))
                seq(V.tensor_reduce(place_f, ohp, AX.X, ALU.add))
                dve.wait_ge(entry_ok, b * 2 + 2)
                own.mark(V.tensor_copy(place[u][:, :], place_f))
                dve.wait_ge(tanh_ok, b + 1)
                v = entry[u][:, :].bitcast(F32).rearrange("p (n c) -> p n c", c=2)[:, :, 1:2]
                V.tensor_scalar(v, top_t.unsqueeze(2), 0.5, 0.5, ALU.mult, ALU.add).then_inc(place_ok, 1)

            def split_h(ev, m, i, p):
                dve.wait_ge(ev_act, ev + 1 + RING)
                dve.wait_ge(y_ps, m + 1)
                hi, lo, v = hhl[i % RING][:, 0, :], hhl[i % RING][:, 1, :], h32[i % RING]
                seq(V.tensor_scalar(hi, v, p[:, 1:2], None, ALU.mult))
                V.scalar_tensor_tensor(out=lo, in0=v, scalar=p[:, 1:2], in1=hi, op0=ALU.mult,
                                       op1=ALU.subtract).then_inc(hhl_ok, 1)

            def sequence(b, u, first=False, last_=False):
                if not last_:
                    dve.wait_ge(stage_used[1], b + 1)
                    scales(b + 1)
                    variances(b + 1, 1 - u)
                if not first:
                    shared_result(b - 1, 1)
                scan_input(b, 0)
                scan(0)
                if not last_:
                    normed(b + 1, 1 - u)
                if last_:
                    places(b, u)
                    tables()
                for i in range(2 * KH):
                    split_h(b * EVENTS + PROJ + i, b * 2 * KH + i, i, PT[:, 0, :])
                    if i == 0:
                        scan_input(b, 1)
                    if i == 1:
                        scan(1)
                    if i == 2 and not last_:
                        places(b, u)
                    if i in (3, 5) and not last_:
                        low_part(b + 1, 0, i // 2 - 1)
                    if i == 4 and not first:
                        dve.wait_ge(o_out, b * 16)
                    if i in (4, 6):
                        residual(b, u, (i - 4) // 2)
                    if i == 9:
                        shared_result(b, 0)
                    if 11 <= i < 16 and not last_:
                        best_two(b + 1, i - 11)
                    if i == 3 and last_:
                        dve.wait_ge(stage_used[1], NW - 1)
                        scales(NW - 1)
                    if 8 <= i < 12 and last_:
                        low_part(NW - 1, (i - 8) // 2, (i - 8) % 2)
                    if i == 13 and last_:
                        keep_entries(0, 0, first=True)
                        parameters(0, 0)

            def keep_entries(n, u, first=False):
                dve.wait_ge(list_in[u], (n - u) * 8 + 16)
                if not first:
                    dve.wait_ge(add_out[u], (n - u) * 16)
                V.tensor_copy(slot_add[u][:, :, :].bitcast(I32),
                              slot_list[u][:, :, :].bitcast(I32)).then_inc(entries_ok, 1)

            def parameters(n, u):
                s = dve.value_load(slot_set[0:1, bass.ds(n, 1)], min_val=0, max_val=NW - 1)
                V.tensor_copy(par[u][:, :], PT[:, bass.ds(s, 1), :].squeeze(1)).then_inc(par_ok, 1)

            def tables():
                own.settle()
                seq(V.tensor_tensor(count, carry, ebase, ALU.subtract))
                seq(V.tensor_scalar(count_i, count, float(ROWS - 1), None, ALU.add))
                seq(V.tensor_scalar(pad_i, count_i, -ROWS, None, ALU.bitwise_and))
                seq(V.tensor_copy(pad, pad_i))
                own.mark(V.tensor_scalar(room, pad, -1.0, float(TOKENS), ALU.mult, ALU.add))
                seq(V.tensor_tensor_scan(pad_end, one, pad, 0.0, ALU.mult, ALU.add))
                seq(V.tensor_tensor(ended, pad_end.unsqueeze(1).to_broadcast([P, SLOTS, E]),
                                    starts.unsqueeze(2).to_broadcast([P, SLOTS, E]), ALU.is_le))
                own.mark(V.tensor_tensor(moved, ended, room.unsqueeze(1).to_broadcast([P, SLOTS, E]), ALU.mult))
                seq(V.tensor_reduce(sets, ended, AX.X, ALU.add))
                seq(V.tensor_scalar(slot_set[:, :], sets, float(E - 1), 1.0, ALU.min, ALU.add))
                seq(V.tensor_reduce(sets, moved, AX.X, ALU.add))
                V.tensor_tensor(slot_at[:, :], sets, starts, ALU.add).then_inc(route_ok, 1)
                dve.wait_ge(route_ok, 1)

            V.engine_nop().then_inc(y_ok, 2)
            V.engine_nop().then_inc(hhl_ok, RING)
            for e in range(E):
                own.mark(V.memset(desc[:, :, e], float(E - e)))
                own.mark(V.memset(ebase[:, e:e + 1], float(e * TOKENS)))
                own.mark(V.memset(carry[:, e:e + 1], float(e * TOKENS)))
            own.mark(V.memset(one, 1.0))
            own.mark(V.memset(scratch, 0.0))
            own.mark(V.memset(b1max, 0.0))
            own.mark(V.memset(PT[:, :, 3:4], 0.0))
            own.settle()
            variances(0, 0)
            normed(0, 0)
            scales(None)
            dve.wait_ge(whi_ok, 1)
            V.scalar_tensor_tensor(out=gw_flat[:, 1, :], in0=graw, scalar=scl[:, 0:1], in1=gw_flat[:, 0, :],
                                   op0=ALU.mult, op1=ALU.subtract).then_inc(gw_ok, 1)
            dve.wait_ge(tab_in, 64)
            V.tensor_reduce(b1max, PT[:, :, 4:NPAR], AX.X, ALU.max, apply_absolute_value=True).then_inc(b1_ok, 1)
            seq(V.tensor_tensor(gb, gb, gb2, ALU.add))
            own.mark(V.tensor_scalar(sbt[:, 0:2], sbt[:, 0:2], 0.5, None, ALU.mult))
            own.mark(V.tensor_scalar(sbt[:, 4:6], sbt[:, 4:6], 0.5, None, ALU.mult))
            dve.wait_ge(iota_ok, 1)
            seq(V.tensor_copy(starts, starts_i))
            V.engine_nop().then_inc(bias_half, 1)
            scales(0)
            for part in range(4):
                low_part(0, part // 2, part % 2)
            for part in range(5):
                best_two(0, part)
            sequence(0, 0, first=True)
            with own.loop(SEQS // 2 - 1, 2 * PER) as it:
                for v in range(2):
                    sequence(it * 2 + 1 + v, (1 + v) % 2)
            sequence(SEQS - 1, 1, last_=True)
            shared_result(SEQS - 1, 1)

            def result(n, u):
                dve.wait_ge(y_ps, (n + 1) * KH + H_A + RING)
                dve.wait_ge(b2_in[u], (n - u) * 8 + 16)
                V.scalar_tensor_tensor(out=chunks(y_sb[u], 2), in0=chunks(ps_y[u][:, :], 2), scalar=par[u][:, 2:3],
                                       in1=b2row[u][:, :].unsqueeze(1).to_broadcast([P, 2, D]), op0=ALU.mult,
                                       op1=ALU.add).then_inc(y_ok, 1)

            def slot(n, u, first=False, final=False):
                for j in range(KH):
                    split_h(n * KH + EV_A + j, n * KH + H_A + j, j, par[u][:, :])
                    if j == 0 and not first:
                        result(n - 1, 1 - u)
                    if j == 3 and not final:
                        parameters(n + 1, 1 - u)
                    if j == 7 and not final:
                        keep_entries(n + 1, 1 - u, first)

            slot(0, 0, first=True)
            with own.loop((SLOTS - 3) // 2, 2 * KH) as it:
                for v in range(2):
                    slot(it * 2 + 1 + v, (1 + v) % 2)
            slot(SLOTS - 2, 1)
            slot(SLOTS - 1, 0, final=True)
            result(SLOTS - 1, 0)

        @block.tensor
        def _(pe):
            T = nc.tensor
            PASSES = ((0, 0), (0, 1), (1, 0))

            def x_transposes(b, i):
                for q in range(2):
                    for t in range(TPB):
                        c = (2 * i + q) * P
                        ins = T.transpose(ps_t16[:, q * SEQ + t * P:q * SEQ + (t + 1) * P], xhl[:, t, c:c + P],
                                          ident[:, :])
                ins.then_inc(xT_ps, 1)

            def logits(b, u):
                pe.wait_ge(xT_ok, b * 2 + 2)
                for t in range(TPB):
                    for n in range(3 * KD):
                        c, (xp, wp) = n // 3, PASSES[n % 3]
                        ins = T.matmul(ps_l[:, t * E:(t + 1) * E], xT[u][:, 2 * xp + c, t * P:(t + 1) * P],
                                       gw[:, wp, c, GATES:GCOL], start=n == 0, stop=n == 3 * KD - 1)
                ins.then_inc(logit_ps, 1)

            def ranks(b):
                pe.wait_ge(top_ok, b + 1)
                for t in range(TPB + 1):
                    for v in range(min(t + 1, TPB)):
                        ins = T.matmul(ps_l[:, 64 + t * E:64 + (t + 1) * E], (before if v == t else ones)[:, :],
                                       mask[:, v * E:(v + 1) * E], start=v == 0, stop=v == min(t, TPB - 1))
                ins.then_inc(rank_ps, 1)

            def scan_transposes(b, i):
                for t in range(2 * i, 2 * i + 2):
                    for ch in range(KD):
                        o = (t % 2) * D + ch * P
                        ins = T.transpose(ps_t[:, o:o + P], tv[ch][:, t * P:(t + 1) * P], identf[:, :])
                ins.then_inc(scanT_ps, 1)

            def projection(b, u, i):
                ch, g = divmod(i, 3)
                pe.wait_ge(ev_act, b * EVENTS + i + 1)
                for n in range(3 * KD):
                    c, (xp, wp) = n // 3, PASSES[n % 3]
                    o = g * D + ch * P
                    ins = T.matmul(ps_e[(2 * u + i) % RING][:, :], gw[:, wp, c, o:o + P], xT[u][:, 2 * xp + c, :],
                                   start=n == 0, stop=n == 3 * KD - 1)
                ins.then_inc(ev_ps, 1)

            def weights(w, o, n):
                return W[:, o:o + n] if w is None else W[:, bass.ds(w + o, n)]

            def layer1(ev, k, j, rhs, w):
                pe.wait_ge(ev_act, ev + 1)
                for n in range(3 * KD):
                    c, (wp, xp) = n // 3, PASSES[n % 3]
                    ins = T.matmul(ps_e[k % RING][:, 0:ROWS], weights(w, wp * HALF + c * H + j * P, P),
                                   rhs[:, 2 * xp + c, :], start=n == 0, stop=n == 3 * KD - 1)
                ins.then_inc(ev_ps, 1)

            def layer2(m, s, i, u, w):
                pe.wait_ge(hhl_ok, m + 1 + RING)
                j = i % KH
                if j == 0:
                    pe.wait_ge(y_ok, s + 1)
                for t in range(2):
                    for hp, wp in PASSES:
                        ins = T.matmul(ps_y[u][:, t * D:(t + 1) * D], hhl[i % RING][:, hp, t * P:(t + 1) * P],
                                       weights(w, (2 + wp) * HALF + j * D, D),
                                       start=(j, t, hp, wp) == (0, 0, 0, 0), stop=(j, hp, wp) == (KH - 1, 1, 0),
                                       skip_group_check=True)
                ins.then_inc(y_ps, 1)

            def make(b, u, k):
                if k < PROJ:
                    projection(b, u, k)
                else:
                    i = k - PROJ
                    s, j = divmod(i, KH)
                    layer1(b * EVENTS + k, 2 * u + k, j, xT[u][:, :, s * ROWS:(s + 1) * ROWS], None)

            def row_transposes(n, u):
                pe.wait_ge(rows_in[u], (n - u) * 16 + 32)
                pe.wait_ge(rowsT_ok, n)
                for q in range(4):
                    for t in range(2):
                        o = q * ROWS + t * P
                        ins = T.transpose(ps_t16[:, o:o + P], xg[u][:, t, q * P:(q + 1) * P], ident[:, :])
                ins.then_inc(rowsT_ps, 1)

            def weight_set(n):
                s = pe.value_load(slot_set[0:1, bass.ds(n, 1)], min_val=0, max_val=NW - 1)
                return pe.snap(s * WSET)

            def sequence(b, u, last_=False):
                for k in range(EVENTS):
                    if k + AHEAD < EVENTS:
                        make(b, u, k + AHEAD)
                    elif not last_:
                        make(b + 1, 1 - u, k + AHEAD - EVENTS)
                    i = k - PROJ
                    if i == 12 and last_:
                        pe.wait_ge(route_ok, 1)
                        pe.wait_ge(r_ok, b * 2 + 2)
                        row_transposes(0, 0)
                    if i >= 14 and last_:
                        if i == 14:
                            pe.wait_ge(stage_used[0], NW)
                            pe.wait_ge(stage_used[1], NW)
                            pe.wait_ge(rowsT_ok, 1)
                        layer1(EV_A + i - 14, i - 14, i - 14, xgT[0], weight_set(0))
                    if i >= 0:
                        layer2(b * 2 * KH + i, b * 2 + i // KH, i, i // KH, None)
                    if k == 1:
                        ranks(b)
                    if i == 3:
                        pe.wait_ge(scan_ok, b * 2 + 2)
                        pe.wait_ge(xT_ok, b * 2 + 2)
                        scan_transposes(b, 0)
                    if i == 5:
                        pe.wait_ge(r_ok, b * 2 + 1)
                        scan_transposes(b, 1)
                    if i == 6 and not last_:
                        pe.wait_ge(xhl_ok, b + 2)
                        pe.wait_ge(r_ok, b * 2 + 2)
                        x_transposes(b + 1, 0)
                    if i == 8 and not last_:
                        pe.wait_ge(xT_ok, b * 2 + 3)
                        x_transposes(b + 1, 1)
                    if i == 10 and not last_:
                        logits(b + 1, 1 - u)

            pe.nop().then_inc(scanT_ps, 2)
            pe.nop().then_inc(y_ps, RING)
            pe.wait_ge(const_ok, 4)
            pe.wait_ge(xhl_ok, 1)
            x_transposes(0, 0)
            pe.wait_ge(xT_ok, 1)
            x_transposes(0, 1)
            pe.wait_ge(gw_ok, 1)
            logits(0, 0)
            for k in range(AHEAD):
                make(0, 0, k)
            pe.wait_ge(stage_used[0], 1)
            pe.wait_ge(stage_used[1], 1)
            with pe.Fori(0, SEQS // 2 - 1) as it:
                for u in range(2):
                    sequence(it * 2 + u, u)
            sequence(SEQS - 2, 0)
            sequence(SEQS - 1, 1, last_=True)

            def slot(n, u, w, final=False):
                w_next = None
                for j in range(KH):
                    if j + AHEAD < KH:
                        layer1(n * KH + EV_A + j + AHEAD, j + AHEAD, j + AHEAD, xgT[u], w)
                    elif not final:
                        i = j + AHEAD - KH
                        if w_next is None:
                            pe.wait_ge(rowsT_ok, n + 2)
                            w_next = weight_set(n + 1)
                        layer1(n * KH + EV_A + j + AHEAD, i, i, xgT[1 - u], w_next)
                    layer2(n * KH + H_A + j, n + S_A, j, u, w)
                    if j == 2 and not final:
                        row_transposes(n + 1, 1 - u)

            layer1(EV_A + 2, 2, 2, xgT[0], weight_set(0))
            with pe.Fori(0, SLOTS // 2) as it:
                for u in range(2):
                    slot(it * 2 + u, u, weight_set(it * 2 + u))
            slot(SLOTS - 1, 0, weight_set(SLOTS - 1), final=True)


def kernel(**inputs):
    import numpy as np
    import concourse.bacc as bacc
    from concourse.bass_utils import run_bass_kernel_spmd

    a = {k.replace("L0_", ""): np.asarray(v) for k, v in inputs.items()}
    b1 = np.concatenate([a["ffn_bs1"][None], a["ffn_b1"]])
    arrays = {
        "x": a["attn_x"].reshape(TOKENS, D),
        "w1": np.concatenate([a["ffn_Ws1"][None], a["ffn_W1"]]).transpose(0, 2, 1),
        "w2": np.concatenate([a["ffn_Ws2"][None], a["ffn_W2"]]).transpose(0, 2, 1),
        "gates": np.concatenate([a["attn_Wg"], a["attn_Wv"], a["attn_Wd"], a["ffn_Wg"].T], axis=1),
        "b1": b1.reshape(NW, KH, P).transpose(2, 0, 1),
        "b2": np.concatenate([a["ffn_bs2"][None], a["ffn_b2"]]),
        "gbias": np.stack([a["ffn_bg"], a["ffn_bias"]]),
        "sbias": np.stack([a["attn_bg"], a["attn_bv"], a["attn_bd"]]).reshape(3 * KD, P).T,
    }
    arrays = {f"in_{k}": np.ascontiguousarray(v) for k, v in arrays.items()}
    nc = bacc.Bacc("TRN2", target_bir_lowering=False, num_devices=1)
    aps = [nc.dram_tensor(k, v.shape, mybir.dt.from_np(v.dtype), kind="ExternalInput").ap() for k, v in arrays.items()]
    out = nc.dram_tensor("out", (TOKENS + ROWS, D), F32, kind="ExternalOutput").ap()
    layer(nc, *aps, out)
    r = run_bass_kernel_spmd(nc, [arrays], core_ids=[0])
    return r.results[0]["out"][:TOKENS].reshape(SEQS, SEQ, D)
```
